# Optimizing a Trainium2 kernel written in Bass

```python
import numpy as np
import jax
import jax.numpy as jnp

def _softmax(x, axis=-1):
    return jax.nn.softmax(x, axis=axis)

def _gelu(x):
    return jax.nn.gelu(x, approximate=True)

def _silu(x):
    return jax.nn.silu(x)

def _sigmoid(x):
    return jax.nn.sigmoid(x)

def _layernorm(x, axis=-1, eps=1e-05):
    m = jnp.mean(x, axis=axis, keepdims=True)
    v = jnp.var(x, axis=axis, keepdims=True)
    return (x - m) / jnp.sqrt(v + eps)

def _scatter_add(tgt, idx, src, axis=0):
    return tgt.at[idx].add(src)

def _segment_sum(src, seg, n):
    return jax.ops.segment_sum(src, seg, n)
kernel_name = 'mk_sandwich_d1_jaxref_r4_07a4d1'

def setup_inputs(seed: int=0):
    np.random.seed(seed)
    _w = jnp.asarray

    def _L0_attn_setup():
        import jax, jax.numpy as jnp
        import numpy as np
        from jax import lax
        BLOCK_LEN = 128
        NEG_INF = -1000000000.0
        key = jax.random.key(seed)
        ks = jax.random.split(key, 8)
        N, L, Dm = (2, 2048, 1024)
        W, H, dh = (256, 16, 64)
        s = lambda fan: 1.0 / np.sqrt(fan)
        return {'inputs': jax.random.normal(ks[0], (N, L, Dm), jnp.float32), 'conv_w': jax.random.normal(ks[1], (3, Dm, 3 * W), jnp.float32) * s(3 * Dm), 'conv_b': jnp.zeros((3 * W,), jnp.float32), 'wq': jax.random.normal(ks[2], (W, H, dh), jnp.float32) * s(W), 'bq': jnp.zeros((H, dh), jnp.float32), 'wk': jax.random.normal(ks[3], (W, H, dh), jnp.float32) * s(W), 'bk': jnp.zeros((H, dh), jnp.float32), 'wv': jax.random.normal(ks[4], (W, H, dh), jnp.float32) * s(W), 'bv': jnp.zeros((H, dh), jnp.float32), 'wo': jax.random.normal(ks[5], (H, dh, W), jnp.float32) * s(H * dh), 'bo': jnp.zeros((W,), jnp.float32), 'proj_w': jax.random.normal(ks[6], (W, Dm), jnp.float32) * s(W), 'proj_b': jnp.zeros((Dm,), jnp.float32)}
    _L0_attn_in = _L0_attn_setup()

    def _L0_ffn_setup():
        import jax, jax.numpy as jnp
        import numpy as np
        LORA_R = 16
        SCALE = 16.0 / np.sqrt(16.0)
        NUM_EXPERTS = 4
        TOP_K = 2
        IN_F = 1024
        OUT_F = 1024
        key = jax.random.key(seed)
        k_x, k_a, k_b, k_r = jax.random.split(key, 4)
        x = jax.random.normal(k_x, (2, 512, IN_F), dtype=jnp.float32)
        A = jax.random.normal(k_a, (NUM_EXPERTS, LORA_R, IN_F), dtype=jnp.float32) * (1.0 / np.sqrt(IN_F))
        B = jax.random.normal(k_b, (NUM_EXPERTS, OUT_F, LORA_R), dtype=jnp.float32) * 0.02
        Wr = jax.random.normal(k_r, (NUM_EXPERTS, IN_F), dtype=jnp.float32) * 0.02
        return {'x': x, 'A': A, 'B': B, 'Wr': Wr}
    _L0_ffn_in = _L0_ffn_setup()
    _d = {'L0_attn_inputs': _L0_attn_in['inputs'], 'L0_attn_conv_w': _L0_attn_in['conv_w'], 'L0_attn_conv_b': _L0_attn_in['conv_b'], 'L0_attn_wq': _L0_attn_in['wq'], 'L0_attn_bq': _L0_attn_in['bq'], 'L0_attn_wk': _L0_attn_in['wk'], 'L0_attn_bk': _L0_attn_in['bk'], 'L0_attn_wv': _L0_attn_in['wv'], 'L0_attn_bv': _L0_attn_in['bv'], 'L0_attn_wo': _L0_attn_in['wo'], 'L0_attn_bo': _L0_attn_in['bo'], 'L0_attn_proj_w': _L0_attn_in['proj_w'], 'L0_attn_proj_b': _L0_attn_in['proj_b'], 'L0_ffn_A': _L0_ffn_in['A'], 'L0_ffn_B': _L0_ffn_in['B'], 'L0_ffn_Wr': _L0_ffn_in['Wr']}
    _x0 = _d['L0_attn_inputs']
    _d['L0_attn_inputs'] = jax.random.normal(jax.random.fold_in(jax.random.key(seed), 1), (4, 512, 1024), dtype=_x0.dtype)
    del _x0
    return _d

def reference(L0_attn_inputs, L0_attn_conv_w, L0_attn_conv_b, L0_attn_wq, L0_attn_bq, L0_attn_wk, L0_attn_bk, L0_attn_wv, L0_attn_bv, L0_attn_wo, L0_attn_bo, L0_attn_proj_w, L0_attn_proj_b, L0_ffn_A, L0_ffn_B, L0_ffn_Wr):

    def _L0_attn_ref(inputs, conv_w, conv_b, wq, bq, wk, bk, wv, bv, wo, bo, proj_w, proj_b):
        import jax, jax.numpy as jnp
        import numpy as np
        from jax import lax
        BLOCK_LEN = 128
        NEG_INF = -1000000000.0
        N, L, Dm = inputs.shape
        x = lax.conv_general_dilated(inputs, conv_w, window_strides=(1,), padding='SAME', dimension_numbers=('NWC', 'WIO', 'NWC')) + conv_b
        q, k, v = jnp.split(x, 3, axis=-1)
        W_ = q.shape[-1]
        nb = L // BLOCK_LEN
        q = q.reshape(N * nb, BLOCK_LEN, W_)
        k = k.reshape(N * nb, BLOCK_LEN, W_)
        v = v.reshape(N * nb, BLOCK_LEN, W_)
        dh = wq.shape[-1]
        qh = jnp.einsum('btd,dhe->bthe', q, wq) + bq
        kh = jnp.einsum('btd,dhe->bthe', k, wk) + bk
        vh = jnp.einsum('btd,dhe->bthe', v, wv) + bv
        scale = 1.0 / jnp.sqrt(jnp.asarray(dh, qh.dtype))
        scores = jnp.einsum('bqhe,bkhe->bhqk', qh * scale, kh)
        causal = jnp.tril(jnp.ones((BLOCK_LEN, BLOCK_LEN), bool))
        scores = jnp.where(causal, scores, NEG_INF)
        p = jax.nn.softmax(scores, axis=-1)
        o = jnp.einsum('bhqk,bkhe->bqhe', p, vh)
        o = jnp.einsum('bqhe,hed->bqd', o, wo) + bo
        o = o.reshape(N, L, W_)
        return o @ proj_w + proj_b

    def _L0_ffn_ref(x, A, B, Wr):
        import jax, jax.numpy as jnp
        import numpy as np
        LORA_R = 16
        SCALE = 16.0 / np.sqrt(16.0)
        NUM_EXPERTS = 4
        TOP_K = 2
        IN_F = 1024
        OUT_F = 1024
        orig_shape = x.shape
        flat = x.reshape(-1, orig_shape[-1])
        logits = flat @ Wr.T
        topk_vals, topk_idx = jax.lax.top_k(logits, TOP_K)
        T = flat.shape[0]
        neg_inf = jnp.finfo(logits.dtype).min
        sparse = jnp.full_like(logits, neg_inf)
        rows = jnp.arange(T)[:, None]
        sparse = sparse.at[rows, topk_idx].set(topk_vals)
        gates = jax.nn.softmax(sparse, axis=-1)
        mid = jnp.einsum('tf,erf->ter', flat, A)
        all_deltas = jnp.einsum('ter,eor->teo', mid, B) * SCALE
        delta = jnp.sum(gates[:, :, None] * all_deltas, axis=1)
        return delta.reshape(*orig_shape[:-1], -1)
    x = L0_attn_inputs
    x = x + _layernorm(_L0_attn_ref(_layernorm(x, axis=-1), L0_attn_conv_w, L0_attn_conv_b, L0_attn_wq, L0_attn_bq, L0_attn_wk, L0_attn_bk, L0_attn_wv, L0_attn_bv, L0_attn_wo, L0_attn_bo, L0_attn_proj_w, L0_attn_proj_b), axis=-1)
    x = x + _layernorm(_L0_ffn_ref(_layernorm(x, axis=-1), L0_ffn_A, L0_ffn_B, L0_ffn_Wr), axis=-1)
    return x

_drawn_inputs = setup_inputs


def setup_inputs(seed=0):
    import zlib

    import numpy as np

    out = dict(_drawn_inputs(seed))
    spreads = {'L0_attn_conv_b': (0.0, 0.1),
     'L0_attn_bq': (0.0, 0.1),
     'L0_attn_bk': (0.0, 0.1),
     'L0_attn_bv': (0.0, 0.1),
     'L0_attn_bo': (0.0, 0.1),
     'L0_attn_proj_b': (0.0, 0.1)}
    factors = {}
    for name, (base, spread) in spreads.items():
        noise = np.random.default_rng([zlib.crc32(name.encode()), seed]).standard_normal(out[name].shape)
        drawn = base * np.exp(spread * noise) if base else spread * noise
        out[name] = jnp.asarray(drawn.astype(out[name].dtype))
    for name, factor in factors.items():
        out[name] = (out[name] * factor).astype(out[name].dtype)
    return out
```

```python
import concourse.bass as bass
from concourse import mybir
from contextlib import ExitStack

F32 = mybir.dt.float32
I32 = mybir.dt.int32
F32R = mybir.dt.float32r
ALU = mybir.AluOpType
ACT = mybir.ActivationFunctionType
AX = mybir.AxisListType

P = 128
NB, L, D = 4, 512, 1024
TB = L // P
KD = D // P
W = 256
KW = W // P
NC = 3 * KW
TAPS = 3
H, DH = 16, 64
HP = H // 2
E, R = 4, 16
ER = E * R
LORA_SCALE = 16.0 / 16.0 ** 0.5
TOP_K = 2
EPS = 1e-5
GUESS = float(0x5F3759DF - 2 ** 31)
NEWTON_STEPS = 3
QK_SCALE = 1.0 / DH ** 0.5
NEG_INF = -1e9 / QK_SCALE
CHUNK = KD * P
RAW_SLOTS, SPLIT_SLOTS = 3, 3
LAG = 3


class Queue:

    def __init__(self, sem, where):
        self.sem, self.where, self.items, self.count = sem, where, [], 0

    def wait(self, *name):
        assert name in self.where, name
        self.items.append(("wait", name))

    def do(self, ins, *names):
        if names:
            self.count += 1
            for n in names:
                assert n not in self.where, n
                self.where[n] = (self.sem, self.count)
        self.items.append(("do", ins, self.sem if names else None, 1))

    def dma(self, out, in_, sem, counts, *names):
        counts[sem.name] = counts.get(sem.name, 0) + 16
        for n in names:
            self.where[n] = (sem, counts[sem.name])
        self.items.append(("do", lambda e: e.dma_start(out, in_), sem, 16))

    def emit(self, eng):
        seen = {}
        for item in self.items:
            if item[0] == "wait":
                sem, value = self.where[item[1]]
                if seen.get(sem.name, 0) < value:
                    eng.wait_ge(sem, value)
                    seen[sem.name] = value
            else:
                ins = item[1](eng)
                if item[2] is not None:
                    ins.then_inc(item[2], item[3])


def build(nc, x, conv_w, wq, wk, wv, wo, proj_w, biases, proj_b, aw, b_t, out):
    with ExitStack() as ctx:
        def sb(name, shape, dt=F32):
            return ctx.enter_context(nc.sbuf_tensor(name, shape, dt))

        def sem(name):
            return ctx.enter_context(nc.semaphore(name))

        ident = sb("ident", [P, P])
        mask = sb("mask", [P, P])
        bias = sb("bias", [P, NC + 3 * HP + KW])
        conv_bias = lambda c: bias[:, c:c + 1]
        head_bias = lambda j, h: bias[:, NC + j * HP + h:NC + j * HP + h + 1]
        out_bias = lambda m: bias[:, NC + 3 * HP + m:NC + 3 * HP + m + 1]
        projb = sb("projb", [P, D])
        aw_sb = sb("aw_sb", [P, KD, ER + E])
        lora_b = [sb(f"lora_b{i}", [P, D], F32R) for i in range(2)]
        raw = [sb(f"raw{i}", [P, CHUNK]) for i in range(RAW_SLOTS)]
        w_hi = [sb(f"w_hi{i}", [P, CHUNK], F32R) for i in range(SPLIT_SLOTS)]
        w_lo = [sb(f"w_lo{i}", [P, CHUNK], F32R) for i in range(SPLIT_SLOTS)]
        xt_hi = sb("xt_hi", [P, KD, L + 2], F32R)
        xt_lo = sb("xt_lo", [P, KD, L + 2], F32R)
        c_hi = sb("c_hi", [P, NC, L], F32R)
        c_lo = sb("c_lo", [P, NC, L], F32R)
        q_t = [sb(f"q_t{i}", [P, L]) for i in range(2)]
        k_t = [sb(f"k_t{i}", [P, L]) for i in range(2)]
        v = sb("v", [P, TB, H * DH])
        prob = [sb(f"prob{i}", [P, 2, TB, P]) for i in range(2)]
        prob_t = [sb(f"prob_t{i}", [P, TB * P]) for i in range(2)]
        top = sb("top", [P, 2, 2, TB])
        ntop = sb("ntop", [P, 2, 2, TB])
        total = sb("total", [P, 2, 2, TB])
        rtotal = sb("rtotal", [P, 2, 2, TB])
        o_hi = [sb(f"o_hi{i}", [P, L], F32R) for i in range(2)]
        o_lo = [sb(f"o_lo{i}", [P, L], F32R) for i in range(2)]
        po_hi = sb("po_hi", [P, KW, L], F32R)
        po_lo = sb("po_lo", [P, KW, L], F32R)
        y = [sb(f"y{t}", [P, D]) for t in range(TB)]
        x1 = [sb(f"x1_{t}", [P, D]) for t in range(TB)]
        x3_t = sb("x3_t", [P, KD, P])
        stats = sb("stats", [P, 2, nc.vector.BN_STATS_DIM])
        mv = sb("mv", [P, TB, 2])
        varp = sb("varp", [P, TB])
        newton = sb("newton", [P, TB])
        rstd = sb("rstd", [P, TB])
        rstd4 = [sb(f"rstd4_{i}", [P, 2]) for i in range(2)]
        logits = sb("logits", [P, E])
        above = sb("above", [P, E, E])
        tied = sb("tied", [P, E, E])
        before = sb("before", [P, E, E])
        rank = sb("rank", [P, E])
        gtop = sb("gtop", [P, 1])
        gexp = sb("gexp", [P, E])
        gate = sb("gate", [P, E])
        gsum = sb("gsum", [P, 1])
        mid = sb("mid", [P, ER])
        mid2 = sb("mid2", [P, 2 * ER], F32R)
        mid_t = sb("mid_t", [P, P], F32R)
        bank = [ctx.enter_context(nc.psum_tensor(f"bank{i}", [P, 512], F32)) for i in range(8)]
        stream_banks, score_banks, turn_banks, wo_banks = bank[0:2], bank[2:4], bank[4:6], bank[6:8]

        where, counts = {}, {}
        pe = Queue(sem("pe_steps"), where)
        act = Queue(sem("act_steps"), where)
        dve = Queue(sem("dve_steps"), where)
        pool = Queue(sem("pool_steps"), where)
        sp = Queue(sem("sp_steps"), where)
        s_raw = [sem(f"s_raw{i}") for i in range(RAW_SLOTS)]
        s_y = [sem(f"s_y{t}") for t in range(TB)]
        s_x1 = [sem(f"s_x1_{t}") for t in range(TB)]
        s_out = [sem(f"s_out{t}") for t in range(TB)]
        s_small = sem("s_small")
        s_lora = sem("s_lora")
        links = [0]

        def link(ins):
            links[0] += 1
            dve.do(ins, ("dve link", links[0]))
            dve.wait("dve link", links[0])

        def mm(dst, lhs, rhs, start, stop, *names):
            pe.do(lambda e: e.matmul(dst, lhs, rhs, start=start, stop=stop), *names)

        def mm3(dst, w_h, w_l, m_h, m_l, start, stop, *names):
            mm(dst, w_h, m_h, start, False)
            mm(dst, w_h, m_l, False, False)
            mm(dst, w_l, m_h, False, stop, *names)

        banks_of = {"stream": stream_banks, "turn": turn_banks, "mid": score_banks, "delta": wo_banks}
        uses = dict.fromkeys(banks_of, 0)

        def take(kind):
            n = uses[kind]
            uses[kind] = n + 1
            if n >= 2:
                pe.wait(kind + " read", n - 2)
            return n, banks_of[kind][n % 2]

        def drained(kind):
            for n in range(max(uses[kind] - 2, 0), uses[kind]):
                pe.wait(kind + " read", n)

        chunks = []
        for b in range(NB):
            for c in range(NC):
                for tap in range(TAPS):
                    src = conv_w[tap].rearrange("(k p) n -> p k n", p=P)[:, :, c * P:(c + 1) * P]
                    chunks.append((("conv", b, c, tap), [(0, KD, src)]))
            for n in range(2):
                src = wv.rearrange("(k p) n -> p k n", p=P)[:, :, n * 512:(n + 1) * 512]
                chunks.append((("v", b, n), [(0, KW, src)]))
            for i in range(HP + LAG):
                parts = []
                if i < HP:
                    for j, w in enumerate((wq, wk)):
                        parts.append((j * KW * P, KW, w.rearrange("(k p) n -> p k n", p=P)[:, :, i * P:(i + 1) * P]))
                if i >= LAG:
                    parts.append((2 * KW * P, 1, wo[(i - LAG) * P:(i - LAG + 1) * P, :].rearrange("p (k n) -> p k n", k=1)))
                chunks.append((("heads", b, i), parts))
            for n in range(2):
                src = proj_w.rearrange("(k p) n -> p k n", p=P)[:, :, n * 512:(n + 1) * 512]
                chunks.append((("proj", b, n), [(0, KW, src)]))
        number = {name: k for k, (name, _) in enumerate(chunks)}
        loaded, split = [0], [0]

        def load_chunks(upto):
            while loaded[0] <= min(upto, len(chunks) - 1):
                k = loaded[0]
                loaded[0] += 1
                if k >= RAW_SLOTS:
                    sp.wait("split hi", k - RAW_SLOTS)
                    sp.wait("split lo", k - RAW_SLOTS)
                for at, kt, src in chunks[k][1]:
                    dst = raw[k % RAW_SLOTS][:, at:at + kt * src.shape[2]].rearrange("p (k n) -> p k n", k=kt)
                    sp.dma(dst, src, s_raw[k % RAW_SLOTS], counts, ("raw", k))

        def split_chunks(upto):
            while split[0] <= min(upto, len(chunks) - 1):
                k = split[0]
                split[0] += 1
                load_chunks(k + 2)
                s = k % SPLIT_SLOTS
                spans = [(at, at + kt * src.shape[2]) for at, kt, src in chunks[k][1]]
                lo, hi = min(a for a, _ in spans), max(z for _, z in spans)
                act.wait("raw", k)
                pool.wait("raw", k)
                if k >= SPLIT_SLOTS:
                    act.wait("chunk used", k - SPLIT_SLOTS)
                act.do(lambda e, k=k, s=s, lo=lo, hi=hi: e.activation(w_hi[s][:, lo:hi], raw[k % RAW_SLOTS][:, lo:hi], ACT.Copy),
                       ("split hi", k))
                pool.wait("split hi", k)
                pool.do(lambda e, k=k, s=s, lo=lo, hi=hi: e.tensor_tensor(
                    w_lo[s][:, lo:hi], raw[k % RAW_SLOTS][:, lo:hi], w_hi[s][:, lo:hi].bitcast(F32), ALU.subtract),
                    ("split lo", k))

        def use_chunk(*name):
            k = number[name]
            split_chunks(number["proj", name[1], 0] + 2 if name[0] == "proj" else k + 2)
            pe.wait("split hi", k)
            pe.wait("split lo", k)
            return k, w_hi[k % SPLIT_SLOTS], w_lo[k % SPLIT_SLOTS]

        def setup():
            sp.dma(bias[:, :], biases, s_small, counts)
            sp.dma(projb[:, :], proj_b, s_small, counts)
            sp.dma(aw_sb[:, :, :], aw.rearrange("(k p) n -> p k n", p=P), s_small, counts, ("small",))
            for half in range(2):
                sp.dma(x1[0][half * ER:(half + 1) * ER, :], b_t, s_lora, counts, ("lora raw",))
            pool.do(lambda e: e.memset(ident[:, :], 0.0), ("ident zero",))
            pool.do(lambda e: e.memset(mask[:, :], 0.0), ("mask zero",))
            pool.wait("ident zero")
            pool.do(lambda e: e.affine_select(out=ident[:, :], in_=ident[:, :], compare_op=ALU.not_equal, fill=1.0,
                                              base=0, pattern=[[-1, P]], channel_multiplier=1), ("ident",))
            pool.wait("mask zero")
            pool.do(lambda e: e.affine_select(out=mask[:, :], in_=mask[:, :], compare_op=ALU.is_ge, fill=NEG_INF,
                                              base=0, pattern=[[-1, P]], channel_multiplier=1), ("mask",))
            for t in (xt_hi, xt_lo):
                for col in (0, L + 1):
                    dve.do(lambda e, t=t, col=col: e.memset(t[:, :, col:col + 1].bitcast(F32), 0.0), ("pad", t.name, col))
            dve.do(lambda e: e.memset(before[:, :, :], 0.0), ("before zero",))
            dve.wait("before zero")
            for i in range(1, E):
                dve.do(lambda e, i=i: e.memset(before[:, i, 0:i], 1.0), ("before", i))

        def lora_weights():
            act.wait("lora raw")
            act.do(lambda e: e.activation(lora_b[0][:, :], x1[0][:, :], ACT.Copy), ("lora hi",))
            dve.wait("lora hi")
            dve.do(lambda e: e.tensor_tensor(lora_b[1][:, :], x1[0][:, :], lora_b[0][:, :].bitcast(F32), ALU.subtract),
                   ("lora lo",))

        def moments(halves, t=0):
            for i, half in enumerate(halves):
                (link if i else dve.do)(lambda e, i=i, half=half: e.bn_stats(stats[:, i, :], half))
            link(lambda e: e.bn_aggr(mv[:, t, :], stats[:, :, :]))

        def inverse_std(n=1):
            r = rstd[:, 0:n]
            link(lambda e: e.tensor_scalar(varp[:, 0:n], mv[:, 0:n, 1], EPS, None, ALU.add))
            link(lambda e: e.tensor_scalar(r.bitcast(I32), varp[:, 0:n].bitcast(I32), -0.5, GUESS, ALU.mult, ALU.add))
            for _ in range(NEWTON_STEPS):
                link(lambda e: e.tensor_tensor(newton[:, 0:n], r, r, ALU.mult))
                link(lambda e: e.scalar_tensor_tensor(out=newton[:, 0:n], in0=newton[:, 0:n], scalar=0.5, in1=varp[:, 0:n],
                                                      op0=ALU.mult, op1=ALU.mult))
                link(lambda e: e.scalar_tensor_tensor(out=r, in0=newton[:, 0:n], scalar=1.5, in1=r,
                                                      op0=ALU.subtract, op1=ALU.mult))

        def scale_row(dst, src, t, *name):
            dve.do(lambda e: e.tensor_scalar(dst[:, :], src[:, :], mv[:, t, 0:1], rstd[:, t:t + 1], ALU.subtract, ALU.mult), name)
            dve.wait(*name)

        def normalise(dst, src, *name):
            moments([src[:, 0:512], src[:, 512:1024]])
            inverse_std()
            scale_row(dst, src, 0, *name)

        def load_x(b, t):
            if b >= 2:
                sp.wait("moe out", b - 2, t)
            sp.dma(y[t][:, :], x[b * TB + t], s_y[t], counts, ("x", b, t))

        def ln1(b):
            for t in range(TB):
                dve.wait("x", b, t)
                moments([y[t][:, 0:512], y[t][:, 512:1024]], t)
            inverse_std(TB)
            for t in range(TB):
                scale_row(y[t], y[t], t, "ln1", b, t)

        def turn_x(b, kt):
            pe.wait("ident")
            n, dst = take("turn")
            for t in range(TB):
                pe.wait("ln1", b, t)
                names = [("x turned", b, kt)] if t == TB - 1 else []
                pe.do(lambda e, t=t: e.transpose(dst[:, t * P:(t + 1) * P], y[t][:, kt * P:(kt + 1) * P], ident[:, :]), *names)
            if b:
                act.wait("conv", b - 1, NC - 1)
            act.wait("x turned", b, kt)
            act.do(lambda e: e.activation(xt_hi[:, kt, 1:L + 1], dst[:, :], ACT.Copy), ("xt hi", b, kt))
            dve.wait("xt hi", b, kt)
            dve.do(lambda e: e.tensor_tensor(xt_lo[:, kt, 1:L + 1], dst[:, :], xt_hi[:, kt, 1:L + 1].bitcast(F32), ALU.subtract),
                   ("xt lo", b, kt), ("turn read", n))

        conv_bank = {}

        def conv(b, c, tap):
            if tap == 0:
                conv_bank[b, c] = take("stream")
            n, acc = conv_bank[b, c]
            k, wh, wl = use_chunk("conv", b, c, tap)
            for kt in range(KD):
                pe.wait("xt lo", b, kt)
                first, last = tap == 0 and kt == 0, tap == TAPS - 1 and kt == KD - 1
                names = [("chunk used", k)] if kt == KD - 1 else []
                names += [("conv", b, c)] if last else []
                cols = slice(kt * P, (kt + 1) * P)
                mm3(acc[:, :], wh[:, cols], wl[:, cols], xt_hi[:, kt, tap:tap + L], xt_lo[:, kt, tap:tap + L],
                    first, last, *names)
            if tap == TAPS - 1:
                if b:
                    act.wait(*(("qk", b - 1, HP - 1) if c < 2 * KW else ("v full", b - 1, 1, TB - 1)))
                split_out(n, acc[:, :], c_hi[:, c, :], c_lo[:, c, :], conv_bias(c), ("conv", b, c), ("c", b, c))

        def split_out(n, acc, hi, lo, bias_col, ready, done):
            act.wait(*ready)
            act.do(lambda e: e.activation(hi, acc, ACT.Identity, bias=bias_col), ("hi of",) + done)
            dve.wait("hi of", *done)
            names = [done] + ([("stream read", n)] if n is not None else [])
            dve.do(lambda e: e.scalar_tensor_tensor(out=lo, in0=acc, scalar=bias_col, in1=hi.bitcast(F32),
                                                    op0=ALU.add, op1=ALU.subtract), *names)

        def project_v(b, n, t):
            k, wh, wl = use_chunk("v", b, n)
            u, acc = take("stream")
            toks = slice(t * P, (t + 1) * P)
            for kt in range(KW):
                c = 2 * KW + kt
                pe.wait("c", b, c)
                names = [("v full", b, n, t)] if kt == KW - 1 else []
                names += [("chunk used", k)] if kt == KW - 1 and t == TB - 1 else []
                cols = slice(kt * 512, (kt + 1) * 512)
                mm3(acc[:, :], c_hi[:, c, toks], c_lo[:, c, toks], wh[:, cols], wl[:, cols], kt == 0, kt == KW - 1, *names)
            act.wait("v full", b, n, t)
            if b:
                act.wait("pv", b - 1, HP - 1)
            act.do(lambda e: e.activation(v[:, t, n * 512:(n + 1) * 512], acc[:, :], ACT.Copy),
                   ("v", b, n, t), ("stream read", u))

        def project_qk(b, h):
            k, wh, wl = use_chunk("heads", b, h)
            for j, dst in enumerate((q_t[h % 2], k_t[h % 2])):
                n, acc = take("stream")
                for kt in range(KW):
                    c = j * KW + kt
                    pe.wait("c", b, c)
                    cols = slice((j * KW + kt) * P, (j * KW + kt + 1) * P)
                    names = [("qk part", b, h, j)] if kt == KW - 1 else []
                    names += [("qk", b, h)] if kt == KW - 1 and j == 1 else []
                    names += [("chunk used", k)] if kt == KW - 1 and j == 1 and h < LAG else []
                    mm3(acc[:, :], wh[:, cols], wl[:, cols], c_hi[:, c, :], c_lo[:, c, :], kt == 0, kt == KW - 1, *names)
                act.wait("qk part", b, h, j)
                if b or h >= 2:
                    act.wait("scores", *back(b, h, 2), 1)
                act.do(lambda e, dst=dst, acc=acc, j=j: e.activation(dst[:, :], acc[:, :], ACT.Identity, bias=head_bias(j, h)),
                       ("qk sb", b, h, j), ("stream read", n))

        def back(b, h, by):
            g = b * HP + h - by
            return g // HP, g % HP

        def scores(b, h):
            s = h % 2
            if h == 0:
                drained("mid")
            for g in range(2):
                rows = slice(g * DH, (g + 1) * DH)
                pe.wait("qk sb", b, h, 0)
                pe.wait("qk sb", b, h, 1)
                if b or h:
                    pe.wait("scores read", *back(b, h, 1), g)
                for t in range(TB):
                    toks = slice(t * P, (t + 1) * P)
                    mm(score_banks[g][:, toks], q_t[s][rows, toks], k_t[s][rows, toks], True, True,
                       *([("scores", b, h, g)] if t == TB - 1 else []))
            for g in range(2):
                dve.wait("scores", b, h, g)
                if b or h >= 2:
                    dve.wait("prob turned", *back(b, h, 2), g)
                for t in range(TB):
                    dve.do(lambda e, g=g, t=t: e.tensor_tensor_reduce(
                        prob[s][:, g, t, :], score_banks[g][:, t * P:(t + 1) * P], mask[:, :], 1.0, NEG_INF * 4,
                        ALU.add, ALU.max, top[:, s, g, t:t + 1]), *([("scores read", b, h, g)] if t == TB - 1 else []))
                dve.wait("scores read", b, h, g)
                dve.do(lambda e, g=g: e.tensor_scalar(ntop[:, s, g, :], top[:, s, g, :], -QK_SCALE, None, ALU.mult),
                       ("ntop", b, h, g))
                act.wait("ntop", b, h, g)
                for t in range(TB):
                    act.do(lambda e, g=g, t=t: e.activation(prob[s][:, g, t, :], prob[s][:, g, t, :], ACT.Exp,
                                                            bias=ntop[:, s, g, t:t + 1], scale=QK_SCALE,
                                                            accum_out=total[:, s, g, t:t + 1]),
                           *([("exp", b, h, g)] if t == TB - 1 else []))

        def probabilities(b, h):
            s = h % 2
            for g in range(2):
                dve.wait("exp", b, h, g)
                dve.do(lambda e, g=g: e.reciprocal(rtotal[:, s, g, :], total[:, s, g, :]), ("rtotal", b, h, g))
                pool.wait("rtotal", b, h, g)
                pool.do(lambda e, g=g: e.tensor_tensor(
                    prob[s][:, g, :, :], prob[s][:, g, :, :],
                    rtotal[:, s, g, :].rearrange("p (t o) -> p t o", o=1).broadcast_to([P, TB, P]), ALU.mult),
                    ("prob", b, h, g))

        def attend(b, h):
            s = h % 2
            for g in range(2):
                n, dst = take("turn")
                pe.wait("prob", b, h, g)
                for t in range(TB):
                    pe.do(lambda e, g=g, t=t, dst=dst: e.transpose(dst[:, t * P:(t + 1) * P], prob[s][:, g, t, :], ident[:, :]),
                          *([("prob turned", b, h, g)] if t == TB - 1 else []))
                act.wait("prob turned", b, h, g)
                if b or h:
                    act.wait("pv part", *back(b, h, 1), g)
                act.do(lambda e, g=g, dst=dst: e.activation(prob_t[g][:, :], dst[:, :], ACT.Copy),
                       ("prob t", b, h, g), ("turn read", n))
            n, acc = take("stream")
            for g in range(2):
                pe.wait("prob t", b, h, g)
                for t in range(TB):
                    pe.wait("v", b, (2 * h + g) * DH // 512, t)
                    names = [("pv part", b, h, g)] if t == TB - 1 else []
                    names += [("pv", b, h)] if t == TB - 1 and g == 1 else []
                    head = (2 * h + g) * DH
                    mm(acc[g * DH:(g + 1) * DH, t * P:(t + 1) * P], v[:, t, head:head + DH],
                       prob_t[g][:, t * P:(t + 1) * P], True, True, *names)
            if b or h >= 2:
                act.wait("wo", *back(b, h, 2))
            split_out(n, acc[:, :], o_hi[s][:, :], o_lo[s][:, :], head_bias(2, h), ("pv", b, h), ("o", b, h))

        def project_wo(b, h):
            k, wh, wl = use_chunk("heads", b, h + LAG)
            pe.wait("o", b, h)
            if h == 0:
                drained("delta")
            for m in range(KW):
                cols = slice(2 * KW * P + m * P, 2 * KW * P + (m + 1) * P)
                names = [("wo", b, h), ("chunk used", k)] if m == KW - 1 else []
                mm3(wo_banks[m][:, :], wh[:, cols], wl[:, cols], o_hi[h % 2][:, :], o_lo[h % 2][:, :],
                    h == 0, h == HP - 1, *names)

        def finish_wo(b):
            for m in range(KW):
                if b:
                    act.wait("proj", b - 1, TB - 1, 1)
                split_out(None, wo_banks[m][:, :], po_hi[:, m, :], po_lo[:, m, :], out_bias(m),
                          ("wo", b, HP - 1), ("po", b, m))

        def project_out(b, t):
            toks = slice(t * P, (t + 1) * P)
            for n in range(2):
                k, wh, wl = use_chunk("proj", b, n)
                u, acc = take("stream")
                for kt in range(KW):
                    pe.wait("po", b, kt)
                    cols = slice(kt * 512, (kt + 1) * 512)
                    names = [("proj", b, t, n)] if kt == KW - 1 else []
                    names += [("chunk used", k)] if kt == KW - 1 and t == TB - 1 else []
                    mm3(acc[:, :], po_hi[:, kt, toks], po_lo[:, kt, toks], wh[:, cols], wl[:, cols],
                        kt == 0, kt == KW - 1, *names)
                dve.wait("proj", b, t, n)
                dve.do(lambda e, n=n, acc=acc: e.tensor_tensor(y[t][:, n * 512:(n + 1) * 512], acc[:, :],
                                                              projb[:, n * 512:(n + 1) * 512], ALU.add),
                       ("attn out", b, t, n), ("stream read", u))

        def load_residual(b, t):
            if b:
                sp.wait("stored", b - 1, t)
            elif t == 0:
                sp.wait("lora hi")
                sp.wait("lora lo")
            sp.dma(x1[t][:, :], x[b * TB + t], s_x1[t], counts, ("residual", b, t))

        def ln23(b, t):
            dve.wait("attn out", b, t, 1)
            normalise(y[t], y[t], "ln2", b, t)
            pool.wait("residual", b, t)
            pool.wait("ln2", b, t)
            pool.do(lambda e: e.tensor_tensor(x1[t][:, :], x1[t][:, :], y[t][:, :], ALU.add), ("x1", b, t))

        def ln3(b, t):
            dve.wait("x1", b, t)
            normalise(y[t], x1[t], "ln3", b, t)

        def turn_x3(b, t):
            pe.wait("ln3", b, t)
            for half in range(2):
                n, dst = take("turn")
                for i in range(4):
                    kt = half * 4 + i
                    pe.do(lambda e, i=i, kt=kt, dst=dst: e.transpose(dst[:, i * P:(i + 1) * P], y[t][:, kt * P:(kt + 1) * P], ident[:, :]),
                          *([("x3 turned", b, t, half)] if i == 3 else []))
                act.wait("x3 turned", b, t, half)
                if b or t:
                    act.wait("mid", *divmod(b * TB + t - 1, TB))
                act.do(lambda e, half=half, dst=dst: e.activation(x3_t[:, half * 4:(half + 1) * 4, :].rearrange("p k n -> p (k n)"),
                                                                  dst[:, :], ACT.Copy),
                       ("x3_t", b, t, half), ("turn read", n))

        def lora_mid(b, t):
            if t == 0:
                for g in range(2):
                    pe.wait("scores read", b, HP - 1, g)
            n, acc = take("mid")
            for kt in range(KD):
                pe.wait("x3_t", b, t, kt // 4)
                mm(acc[:, 0:ER + E], x3_t[:, kt, :], aw_sb[:, kt, :], kt == 0, kt == KD - 1,
                   *([("mid", b, t)] if kt == KD - 1 else []))
            dve.wait("mid", b, t)
            if b or t:
                dve.wait("gexp", *divmod(b * TB + t - 1, TB))
            dve.do(lambda e: e.tensor_copy(mid[:, :], acc[:, 0:ER]), ("mid sb", b, t))
            dve.do(lambda e: e.tensor_copy(logits[:, :], acc[:, ER:ER + E]), ("logits", b, t), ("mid read", n))
            dve.wait("logits", b, t)
            dve.do(lambda e: e.tensor_reduce(gtop[:, :], logits[:, :], AX.X, ALU.max, negate=True), ("gtop", b, t))
            act.wait("gtop", b, t)
            act.do(lambda e: e.activation(gexp[:, :], logits[:, :], ACT.Exp, bias=gtop[:, 0:1]), ("gexp", b, t))
            own = logits[:, :].rearrange("p (i o) -> p i o", o=1).broadcast_to([P, E, E])
            other = logits[:, :].rearrange("p (o j) -> p o j", o=1).broadcast_to([P, E, E])
            dve.do(lambda e: e.tensor_tensor(above[:, :, :], other, own, ALU.is_gt), ("above", b, t))
            link(lambda e: e.tensor_tensor(tied[:, :, :], other, own, ALU.is_equal))
            link(lambda e: e.tensor_tensor(tied[:, :, :], tied[:, :, :], before[:, :, :], ALU.mult))
            link(lambda e: e.tensor_tensor(above[:, :, :], above[:, :, :], tied[:, :, :], ALU.add))
            link(lambda e: e.tensor_reduce(rank[:, :], above[:, :, :], AX.X, ALU.add))
            dve.wait("gexp", b, t)
            link(lambda e: e.scalar_tensor_tensor(out=gate[:, :], in0=rank[:, :], scalar=float(TOP_K), in1=gexp[:, :],
                                                  op0=ALU.is_lt, op1=ALU.mult))
            link(lambda e: e.tensor_reduce(gsum[:, :], gate[:, :], AX.X, ALU.add))
            link(lambda e: e.reciprocal(gsum[:, :], gsum[:, :]))
            link(lambda e: e.tensor_scalar(gate[:, :], gate[:, :], gsum[:, 0:1], LORA_SCALE, ALU.mult, ALU.mult))
            link(lambda e: e.tensor_tensor(mid[:, :].rearrange("p (e r) -> p e r", r=R), mid[:, :].rearrange("p (e r) -> p e r", r=R),
                                           gate[:, :].rearrange("p (e o) -> p e o", o=1).broadcast_to([P, E, R]), ALU.mult))
            if b or t:
                dve.wait("mid turned", *divmod(b * TB + t - 1, TB))
            link(lambda e: e.tensor_copy(mid2[:, 0:ER], mid[:, :]))
            dve.do(lambda e: e.tensor_tensor(mid2[:, ER:2 * ER], mid[:, :], mid2[:, 0:ER].bitcast(F32), ALU.subtract),
                   ("mid2", b, t))

        def lora_out(b, t):
            n, dst = take("turn")
            pe.wait("mid2", b, t)
            pe.do(lambda e: e.transpose(dst[:, 0:P], mid2[:, :].bitcast(F32), ident[:, :]), ("mid turned", b, t))
            act.wait("mid turned", b, t)
            if b or t:
                act.wait("delta", *divmod(b * TB + t - 1, TB))
            act.do(lambda e: e.activation(mid_t[:, :], dst[:, 0:P], ACT.Copy), ("mid_t", b, t), ("turn read", n))
            pe.wait("mid_t", b, t)
            pe.wait("lora lo")
            accs = []
            for j in range(2):
                pe.wait("po", b, j)
                u, acc = take("delta")
                accs.append((u, acc))
                cols = slice(j * 512, (j + 1) * 512)
                mm(acc[:, :], mid_t[:, :], lora_b[0][:, cols], True, False)
                mm(acc[:, :], mid_t[:, :], lora_b[1][:, cols], False, True, ("delta half", b, t, j), *([("delta", b, t)] if j else []))
            r4 = rstd4[t % 2]
            dve.wait("delta", b, t)
            if b or t >= 2:
                dve.wait("moe norm", *divmod(b * TB + t - 2, TB), 1)
            moments([acc[:, :] for _, acc in accs])
            inverse_std()
            dve.do(lambda e: e.tensor_copy(r4[:, 0:1], rstd[:, 0:1]))
            dve.do(lambda e: e.tensor_scalar(r4[:, 1:2], mv[:, 0, 0:1], rstd[:, 0:1], -1.0, ALU.mult, ALU.mult), ("rstd4", b, t))
            act.wait("rstd4", b, t)
            for j, (u, acc) in enumerate(accs):
                act.do(lambda e, j=j, acc=acc: e.activation(y[t][:, j * 512:(j + 1) * 512], acc[:, :], ACT.Identity,
                                                            bias=r4[:, 1:2], scale=r4[:, 0:1]),
                       ("moe norm", b, t, j), ("delta read", u))
            pool.wait("moe norm", b, t, 1)
            pool.do(lambda e: e.tensor_tensor(x1[t][:, :], x1[t][:, :], y[t][:, :], ALU.add), ("moe out", b, t))
            sp.wait("moe out", b, t)
            sp.dma(out[b * TB + t], x1[t][:, :], s_out[t], counts, ("stored", b, t))

        for t in range(TB):
            load_x(0, t)
        setup()
        split_chunks(0)
        for q in (act, dve):
            q.wait("small")
        ln1(0)
        for kt in range(KD):
            turn_x(0, kt)
        lora_weights()
        dve.wait("mask")

        for b in range(NB):
            for c in range(NC):
                for tap in range(TAPS):
                    conv(b, c, tap)
                    at = c * TAPS + tap
                    if b:
                        if at % 4 == 0 and at // 4 < TB:
                            ln3(b - 1, at // 4)
                        if at % 4 == 1 and at // 4 < TB:
                            turn_x3(b - 1, at // 4)
                        if at % 4 == 2 and at // 4 < TB:
                            lora_mid(b - 1, at // 4)
                        if at >= 4 and at % 4 == 0:
                            lora_out(b - 1, at // 4 - 1)
            for t in range(TB):
                load_residual(b, t)
                if b + 1 < NB:
                    load_x(b + 1, t)
            for n in range(2):
                for t in range(TB):
                    project_v(b, n, t)
            if b + 1 < NB:
                ln1(b + 1)
            for i in range(HP + LAG):
                if 1 <= i <= HP:
                    scores(b, i - 1)
                if i < HP:
                    project_qk(b, i)
                if 1 <= i <= HP and b + 1 < NB:
                    turn_x(b + 1, i - 1)
                if 1 <= i <= HP:
                    probabilities(b, i - 1)
                if 2 <= i < HP + 2:
                    attend(b, i - 2)
                if i >= LAG:
                    project_wo(b, i - LAG)
            finish_wo(b)
            for t in range(TB):
                project_out(b, t)
                ln23(b, t)
        b = NB - 1
        for t in range(TB):
            ln3(b, t)
            turn_x3(b, t)
            lora_mid(b, t)
            lora_out(b, t)
        for t in range(TB):
            sp.wait("stored", b, t)

        with nc.Block() as block:
            block.tensor(pe.emit)
            block.scalar(act.emit)
            block.vector(dve.emit)
            block.gpsimd(pool.emit)
            block.sync(sp.emit)


def kernel(**inputs):
    import numpy as np
    import concourse.bacc as bacc
    from concourse.bass_utils import run_bass_kernel_spmd

    g = {k.replace("L0_attn_", "").replace("L0_ffn_", ""): np.asarray(a) for k, a in inputs.items()}
    flat = lambda a, *s: np.ascontiguousarray(a.reshape(*s))
    columns = lambda a: a.reshape(-1, P).T
    arrays = {
        "x": flat(g["inputs"], NB * TB, P, D),
        "conv_w": flat(g["conv_w"], TAPS, D, 3 * W),
        "wq": flat(g["wq"], W, H * DH),
        "wk": flat(g["wk"], W, H * DH),
        "wv": flat(g["wv"], W, H * DH),
        "wo": flat(g["wo"], H * DH, W),
        "proj_w": flat(g["proj_w"], W, D),
        "biases": np.ascontiguousarray(np.concatenate([columns(g[n]) for n in ("conv_b", "bq", "bk", "bv", "bo")], axis=1)),
        "proj_b": np.ascontiguousarray(np.broadcast_to(g["proj_b"], (P, D))),
        "aw": np.ascontiguousarray(np.concatenate([g["A"].reshape(ER, D).T, g["Wr"].T], axis=1)),
        "b_t": np.ascontiguousarray(g["B"].transpose(0, 2, 1).reshape(ER, D)),
    }
    nc = bacc.Bacc("TRN2", target_bir_lowering=False, num_devices=1)
    aps = {n: nc.dram_tensor(n, a.shape, mybir.dt.from_np(a.dtype), kind="ExternalInput").ap() for n, a in arrays.items()}
    out = nc.dram_tensor("out", (NB * TB, P, D), F32, kind="ExternalOutput").ap()
    build(nc, out=out, **aps)
    result = run_bass_kernel_spmd(nc, [arrays], core_ids=[0]).results[0]["out"]
    return result.reshape(NB, L, D)
```

```python
import concourse.bass as bass
from concourse import mybir
from contextlib import ExitStack

F32 = mybir.dt.float32
I32 = mybir.dt.int32
F32R = mybir.dt.float32r
ALU = mybir.AluOpType
ACT = mybir.ActivationFunctionType
AX = mybir.AxisListType

P = 128
NB, L, D = 4, 512, 1024
TB = L // P
KD = D // P
W = 256
KW = W // P
NC = 3 * KW
C_ORDER = [4, 5, 0, 1, 2, 3]
TAPS = 3
FILT = 4
J_ORDER = [0, 3, 1, 2]
L2 = L // 2
H, DH = 16, 64
HP = H // 2
E, R = 4, 16
ER = E * R
LORA_SCALE = 16.0 / 16.0 ** 0.5
TOP_K = 2
EPS = 1e-5
GUESS = float(0x5F3759DF - 2 ** 31 - 2 ** 22)
NEWTON_STEPS = 3
QK_SCALE = 1.0 / DH ** 0.5
NEG_INF = -1e9 / QK_SCALE
CHUNK = 512
HALF = CHUNK // P
HALVES = KD // HALF
SLOTS = FILT * HALVES
RAW_SLOTS, SPLIT_SLOTS = 5, 6
SUM_LEAD = 1
LOW_TURN = {True: 2, False: 3}
LEAD = 4
LAG = 3


class Queue:

    def __init__(self, sem, where):
        self.sem, self.where, self.items, self.count = sem, where, [], 0

    def wait(self, *name):
        assert name in self.where, name
        self.items.append(("wait", name))

    def do(self, ins, *names):
        if names:
            self.count += 1
            for n in names:
                assert n not in self.where, n
                self.where[n] = (self.sem, self.count)
        self.items.append(("do", ins, self.sem if names else None, 1))

    def dma(self, out, in_, sem, counts, *names):
        counts[sem.name] = counts.get(sem.name, 0) + 16
        for n in names:
            self.where[n] = (sem, counts[sem.name])
        self.items.append(("do", lambda e: e.dma_start(out, in_), sem, 16))

    def emit(self, eng):
        seen = {}
        for item in self.items:
            if item[0] == "wait":
                sem, value = self.where[item[1]]
                if seen.get(sem.name, 0) < value:
                    eng.wait_ge(sem, value)
                    seen[sem.name] = value
            else:
                ins = item[1](eng)
                if item[2] is not None:
                    ins.then_inc(item[2], item[3])


def build(nc, x, conv_w, wq, wk, wv, wo, proj_w, biases, proj_b, aw, b_t, out):
    with ExitStack() as ctx:
        def sb(name, shape, dt=F32):
            return ctx.enter_context(nc.sbuf_tensor(name, shape, dt))

        def sem(name):
            return ctx.enter_context(nc.semaphore(name))

        ident = sb("ident", [P, P])
        mask = sb("mask", [P, P])
        bias = sb("bias", [P, NC + 3 * HP + KW])
        conv_bias = lambda c: bias[:, c:c + 1]
        head_bias = lambda j, h: bias[:, NC + j * HP + h:NC + j * HP + h + 1]
        out_bias = lambda m: bias[:, NC + 3 * HP + m:NC + 3 * HP + m + 1]
        projb = sb("projb", [P, D])
        aw_sb = sb("aw_sb", [P, KD, ER + E])
        lora_b = [sb(f"lora_b{i}", [P, D], F32R) for i in range(2)]
        raw_slots = [sb(f"raw{i}", [P, CHUNK]) for i in range(RAW_SLOTS)]
        w_hi = [sb(f"w_hi{i}", [P, CHUNK], F32R) for i in range(SPLIT_SLOTS)]
        w_lo = [sb(f"w_lo{i}", [P, CHUNK], F32R) for i in range(SPLIT_SLOTS)]
        xt = [sb(f"xt{i}", [P, L + 2]) for i in range(2)]
        filt = sb("filt", [P, FILT, L2])
        f_hi = sb("f_hi", [P, KD, FILT, L2], F32R)
        f_lo = sb("f_lo", [P, KD, FILT, L2], F32R)
        c_hi = sb("c_hi", [P, NC, L], F32R)
        c_lo = sb("c_lo", [P, NC, L], F32R)
        q_t = sb("q_t", [P, L])
        k_t = sb("k_t", [P, L])
        v = sb("v", [P, TB, H * DH])
        prob = sb("prob", [P, 2, TB, P])
        prob_t = sb("prob_t", [P, 2, TB * P])
        top = sb("top", [P, 2, TB])
        ntop = sb("ntop", [P, 2, TB])
        total = sb("total", [P, 2, TB])
        rtotal = sb("rtotal", [P, 2, TB])
        o_hi = sb("o_hi", [P, L], F32R)
        o_lo = sb("o_lo", [P, L], F32R)
        po_hi = sb("po_hi", [P, KW, L], F32R)
        po_lo = sb("po_lo", [P, KW, L], F32R)
        work = [sb(f"work{t}", [P, D]) for t in range(TB)]
        y = [v[:, t, :] for t in range(TB)]
        x3_t = prob_t[:, :, :].rearrange("p g (k n) -> p (g k) n", n=P)
        m12 = q_t[:, :].rearrange("p (j n) -> p j n", j=2)
        m12_sums = k_t[:, :].rearrange("p (j n) -> p j n", j=2)
        conv_out = prob[:, 0, :, :].rearrange("p t n -> p (t n)")
        tap1, outer, inner = v[:, 1, :], v[:, 2, :], v[:, 3, :]
        sums = [v[:, 0, :], filt[:, :, :].rearrange("p j n -> p (j n)")]
        sums = [s[:, a:a + CHUNK] for s in sums for a in (0, CHUNK)]
        norms = {}
        for name in ("ln1", "ln2", "ln3", "ln4"):
            norms[name] = (sb(name + "_mv", [P, TB, 2]), sb(name + "_r", [P, TB]), sb(name + "_nmr", [P, TB]))
        stats = sb("stats", [P, TB, 2, nc.vector.BN_STATS_DIM])
        varh = sb("varh", [P, TB])
        newton = sb("newton", [P, TB])
        PR = 2
        logits = sb("logits", [P, PR, E])
        above = sb("above", [P, PR, E, E])
        tied = sb("tied", [P, PR, E, E])
        before = sb("before", [P, PR, E, E])
        rank = sb("rank", [P, PR, E])
        gtop = sb("gtop", [P, PR])
        gexp = sb("gexp", [P, PR, E])
        gate = sb("gate", [P, PR, E])
        gsum = sb("gsum", [P, PR])
        mid = sb("mid", [P, PR, ER])
        mid2 = sb("mid2", [P, PR, 2 * ER], F32R)
        mid_t = sb("mid_t", [P, PR, P], F32R)
        bank = [ctx.enter_context(nc.psum_tensor(f"bank{i}", [P, 512], F32)) for i in range(8)]
        score_banks, wo_banks = bank[2:4], bank[6:8]
        conv_banks = [bank[2:4], bank[0:2]]
        banks_of = {
            "stream": bank[0:2],
            "v": bank[2:4],
            "turn": bank[4:6],
            "side": bank[6:8],
        }

        where, counts = {}, {}
        pe = Queue(sem("pe_steps"), where)
        act = Queue(sem("act_steps"), where)
        dve = Queue(sem("dve_steps"), where)
        pool = Queue(sem("pool_steps"), where)
        sp = Queue(sem("sp_steps"), where)
        s_raw = [sem(f"s_raw{i}") for i in range(RAW_SLOTS)]
        s_store = [sem(f"s_store{i}") for i in range(len(sums))]
        s_work = [sem(f"s_work{t}") for t in range(TB)]
        s_out = [sem(f"s_out{t}") for t in range(TB)]
        s_tap1 = sem("s_tap1")
        s_small = sem("s_small")
        s_lora = sem("s_lora")
        links = [0]

        def link(ins):
            links[0] += 1
            dve.do(ins, ("dve link", links[0]))
            dve.wait("dve link", links[0])

        def mm(dst, lhs, rhs, start, stop, *names):
            pe.do(lambda e: e.matmul(dst, lhs, rhs, start=start, stop=stop), *names)

        def mm3(dst, w_h, w_l, m_h, m_l, start, stop, *names):
            mm(dst, w_h, m_h, start, False)
            mm(dst, w_h, m_l, False, False)
            mm(dst, w_l, m_h, False, stop, *names)

        uses = dict.fromkeys(banks_of, 0)

        def take(kind):
            n = uses[kind]
            uses[kind] = n + 1
            if n >= 2:
                pe.wait(kind + " read", n - 2)
            return n, banks_of[kind][n % 2]

        def drained(kind):
            for n in range(max(uses[kind] - 2, 0), uses[kind]):
                pe.wait(kind + " read", n)

        summed = nc.dram_tensor("summed_filters", (NC, 2, HALVES, P, CHUNK), F32, kind="Internal").ap()

        def tap_half(tap, c, half):
            rows = slice(half * HALF * P, (half + 1) * HALF * P)
            return conv_w[tap, rows, c * P:(c + 1) * P].rearrange("(k p) n -> p k n", p=P)

        chunks = []

        def conv_chunk(b, c, j, half):
            if j == 0:
                parts = [(0, tap_half(0, c, half))]
            elif j == 3:
                parts = [(0, tap_half(2, c, half))]
            else:
                parts = [(0, summed[c, j - 1, half].rearrange("p (k n) -> p k n", k=HALF))] if b else []
            return ("conv", b, c, j, half), CHUNK, parts

        def columns_of(w, at, n):
            return w[:, at:at + n].rearrange("(k p) n -> p k n", p=P)

        def row_tile(w, kt, at, n):
            return w[kt * P:(kt + 1) * P, at:at + n].rearrange("p (k n) -> p k n", k=1)

        def plan_chunks(order):
            for name in order:
                kind, b = name[0], name[1]
                if kind == "conv":
                    chunks.append(conv_chunk(*name[1:]))
                elif kind == "v":
                    chunks.append((name, CHUNK, [(0, row_tile(wv, name[3], name[2] * 512, 512))]))
                elif kind == "proj":
                    chunks.append((name, CHUNK, [(0, row_tile(proj_w, name[4], name[3] * 512, 512))]))
                elif kind == "qk":
                    chunks.append((name, CHUNK, [(j * KW * P, columns_of(w, name[2] * P, P)) for j, w in enumerate((wq, wk))]))
                elif kind == "wo":
                    chunks.append((name, KW * P, [(0, row_tile(wo, name[2], 0, KW * P))]))

        number = {}
        loaded, split, summed_upto = [0], [0], [0]
        raw, in_raw, summing = {}, [], []

        clock, pending = [0], []

        def later(ticks, step):
            pending.append((clock[0] + ticks, step))

        def tick():
            clock[0] += 1
            due = [p for p in pending if p[0] <= clock[0]]
            pending[:] = [p for p in pending if p[0] > clock[0]]
            for _, step in due:
                step()

        def settle():
            while pending:
                tick()

        def load_chunks():
            while loaded[0] < len(chunks):
                k = loaded[0]
                name, _, parts = chunks[k]
                if parts:
                    n = len(in_raw)
                    last = in_raw[n - RAW_SLOTS] if n >= RAW_SLOTS else None
                    if last is not None and ("split lo", last) not in where:
                        break
                    if name[:2] == ("conv", 0) and name[3:] == (0, 0) and not tap1_free(name[2]):
                        break
                    if last is not None:
                        sp.wait("split hi", last)
                        sp.wait("split lo", last)
                        if chunks[last][0][:2] == ("conv", 0):
                            sp.wait("kept", last)
                    in_raw.append(k)
                    slot = raw[k] = raw_slots[n % RAW_SLOTS]
                    for at, src in parts:
                        kt, cols = src.shape[1], src.shape[2]
                        sp.dma(slot[:, at:at + kt * cols].rearrange("p (k n) -> p k n", k=kt), src,
                               s_raw[n % RAW_SLOTS], counts, ("raw", k))
                loaded[0] += 1
                if name[:2] == ("conv", 0) and name[3:] == (0, 0):
                    load_tap1(name[2])

        def tap1_free(c):
            return c == C_ORDER[0] or ("inner", C_ORDER[C_ORDER.index(c) - 1]) in where

        def load_tap1(c):
            if c != C_ORDER[0]:
                sp.wait("inner", C_ORDER[C_ORDER.index(c) - 1])
            for h in range(HALVES):
                sp.dma(tap1[:, h * CHUNK:(h + 1) * CHUNK].rearrange("p (k n) -> p k n", k=HALF), tap_half(1, c, h),
                       s_tap1, counts, ("tap1", c))

        def sum_filters(k, c, j, half):
            cols = slice(half * CHUNK, (half + 1) * CHUNK)
            if j == 0:
                dve.wait("raw", k)
                if summing:
                    dve.wait("raw", summing[-1])
                dve.do(lambda e: e.tensor_copy(outer[:, cols], raw[k][:, :]), ("kept", k))
            elif j == 3:
                dve.wait("raw", k)
                dve.wait("kept", number["conv", 0, c, 0, half])
                dve.do(lambda e: e.tensor_tensor(outer[:, cols], outer[:, cols], raw[k][:, :], ALU.add), ("outer", c, half), ("kept", k))
                if half == HALVES - 1:
                    dve.wait("tap1", c)
                    dve.do(lambda e: e.tensor_scalar(inner, tap1, 0.5, None, ALU.mult), ("inner", c))
            else:
                s = len(summing)
                summing.append(k)
                dst = sums[s % len(sums)]
                raw[k] = dst
                if s >= len(sums):
                    for reader in ("kept", "split hi", "split lo"):
                        dve.wait(reader, summing[s - len(sums)])
                else:
                    for kt in (KD - 2, KD - 1):
                        dve.wait("f lo", 0, kt)
                dve.wait("outer", c, half)
                dve.wait("inner", c)
                dve.do(lambda e: e.scalar_tensor_tensor(out=dst, in0=outer[:, cols], scalar=0.5, in1=inner[:, cols],
                                                        op0=ALU.mult, op1=ALU.add if j == 1 else ALU.subtract), ("raw", k))
                sp.wait("raw", k)
                sp.dma(summed[c, j - 1, half], dst, s_store[s % len(sums)], counts, ("kept", k))

        def split_chunks(upto):
            load_chunks()
            while summed_upto[0] <= min(upto + SUM_LEAD, len(chunks) - 1):
                k = summed_upto[0]
                summed_upto[0] += 1
                if chunks[k][0][:2] == ("conv", 0):
                    sum_filters(k, *chunks[k][0][2:])
            while split[0] <= min(upto, len(chunks) - 1):
                k = split[0]
                split[0] += 1
                name, n, _ = chunks[k]
                src, hi, lo = raw[k][:, 0:n], w_hi[k % SPLIT_SLOTS][:, 0:n], w_lo[k % SPLIT_SLOTS][:, 0:n]
                if k >= SPLIT_SLOTS:
                    act.wait("chunk used", k - SPLIT_SLOTS)
                low = dve if k % LOW_TURN[name[0] == "conv"] == 0 else pool
                act.wait("raw", k)
                act.do(lambda e, hi=hi, src=src: e.activation(hi, src, ACT.Copy), ("split hi", k))
                low.wait("split hi", k)
                low.do(lambda e, lo=lo, hi=hi, src=src: e.tensor_tensor(lo, src, hi.bitcast(F32), ALU.subtract), ("split lo", k))
                load_chunks()

        def use_chunk(*name):
            k = number[name]
            split_chunks(k + LEAD)
            pe.wait("split hi", k)
            pe.wait("split lo", k)
            return k, w_hi[k % SPLIT_SLOTS], w_lo[k % SPLIT_SLOTS]

        def setup():
            sp.dma(bias[:, :], biases, s_small, counts)
            sp.dma(projb[:, :], proj_b, s_small, counts)
            sp.dma(aw_sb[:, :, :], aw.rearrange("(k p) n -> p k n", p=P), s_small, counts, ("small",))
            for half in range(2):
                sp.dma(prob[half * ER:(half + 1) * ER, :, :, :].rearrange("p g t n -> p (g t n)"), b_t,
                       s_lora, counts, ("lora raw",))

        def constants():
            pool.do(lambda e: e.memset(ident[:, :], 0.0), ("ident zero",))
            pool.do(lambda e: e.memset(mask[:, :], 0.0), ("mask zero",))
            pool.wait("ident zero")
            pool.do(lambda e: e.affine_select(out=ident[:, :], in_=ident[:, :], compare_op=ALU.not_equal, fill=1.0,
                                              base=0, pattern=[[-1, P]], channel_multiplier=1), ("ident",))
            pool.wait("mask zero")
            pool.do(lambda e: e.affine_select(out=mask[:, :], in_=mask[:, :], compare_op=ALU.is_ge, fill=NEG_INF,
                                              base=0, pattern=[[-1, P]], channel_multiplier=1), ("mask",))
            for i in range(2):
                for col in (0, L + 1):
                    pool.do(lambda e, i=i, col=col: e.memset(xt[i][:, col:col + 1], 0.0), ("pad", i, col))
            pool.do(lambda e: e.memset(before[:, :, :, :], 0.0), ("before zero",))
            pool.wait("before zero")
            for i in range(1, E):
                pool.do(lambda e, i=i: e.memset(before[:, :, i, 0:i], 1.0), ("before", i))

        def lora_weights():
            src = prob[:, :, :, :].rearrange("p g t n -> p (g t n)")
            act.wait("lora raw")
            act.do(lambda e: e.activation(lora_b[0][:, :], src, ACT.Copy), ("lora hi",))
            dve.wait("lora hi")
            dve.do(lambda e: e.tensor_tensor(lora_b[1][:, :], src, lora_b[0][:, :].bitcast(F32), ALU.subtract), ("lora lo",))

        def inverse_std(norm, b, t0, n):
            mv, rr, nmr = norms[norm]
            ts = slice(t0, t0 + n)
            for t in range(t0, t0 + n):
                dve.wait("stats", norm, b, t, 1)
            for t in range(t0, t0 + n):
                (link if t == t0 + n - 1 else dve.do)(lambda e, t=t: e.bn_aggr(mv[:, t, :], stats[:, t, :, :]))
            r, h, u = rr[:, ts], varh[:, ts], newton[:, ts]
            link(lambda e: e.tensor_scalar(h, mv[:, ts, 1], EPS, 0.5, ALU.add, ALU.mult))
            link(lambda e: e.tensor_scalar(r.bitcast(I32), h.bitcast(I32), -0.5, GUESS, ALU.mult, ALU.add))
            for _ in range(NEWTON_STEPS):
                link(lambda e: e.tensor_tensor(u, r, r, ALU.mult))
                link(lambda e: e.tensor_tensor(u, u, h, ALU.mult))
                link(lambda e: e.scalar_tensor_tensor(out=r, in0=u, scalar=1.5, in1=r, op0=ALU.subtract, op1=ALU.mult))
            dve.do(lambda e: e.scalar_tensor_tensor(out=nmr[:, ts], in0=mv[:, ts, 0], scalar=-1.0, in1=r,
                                                    op0=ALU.mult, op1=ALU.mult), (norm, b, t0, "std"))

        def scale_row(norm, b, t0, t, dst, src, *names):
            _, rr, nmr = norms[norm]
            act.wait(norm, b, t0, "std")
            act.do(lambda e: e.activation(dst, src, ACT.Identity, bias=nmr[:, t:t + 1], scale=rr[:, t:t + 1]), *names)

        def row_stats(norm, b, t, halves):
            for i, half in enumerate(halves):
                dve.do(lambda e, i=i, half=half: e.bn_stats(stats[:, t, i, :], half), ("stats", norm, b, t, i))

        def load_x(b, t):
            if b >= 2:
                sp.wait("stored", b - 2, t)
            sp.dma(work[t][:, :], x[b * TB + t], s_work[t], counts, ("x", b, t))

        def next_x(b, t):
            if b + 2 < NB:
                load_x(b + 2, t)

        def ln1(b):
            for t in range(TB):
                dve.wait("x", b, t)
                row_stats("ln1", b, t, [work[t][:, 0:512], work[t][:, 512:1024]])
            inverse_std("ln1", b, 0, TB)
            for t in range(TB):
                scale_row("ln1", b, 0, t, work[t][:, :], work[t][:, :], ("ln1", b, t))

        def turn_x(b, kt):
            i = kt % 2
            buf = v[:, 0, :].rearrange("p (j n) -> p j n", j=FILT) if b == 0 and i else filt[:, :, :]
            pe.wait("ident")
            n, dst = take("turn")
            for t in range(TB):
                pe.wait("ln1", b, t)
                names = [("x turned", b, kt)] if t == TB - 1 else []
                pe.do(lambda e, t=t: e.transpose(dst[:, t * P:(t + 1) * P], work[t][:, kt * P:(kt + 1) * P], ident[:, :]), *names)
            act.wait("x turned", b, kt)
            if b or kt >= 2:
                for j in range(FILT):
                    act.wait("filt", *back(KD, b, kt, 2), j)
            act.do(lambda e: e.activation(xt[i][:, 1:L + 1], dst[:, :], ACT.Copy), ("xt", b, kt), ("turn read", n))
            d = [xt[i][:, a:a + L - 1:2] for a in range(4)]
            terms = [(0, 2, ALU.subtract), (1, 2, ALU.add), (2, 1, ALU.subtract), (1, 3, ALU.subtract)]
            for j, (p, q, op) in enumerate(terms):
                eng = dve if j >= 2 else pool
                eng.wait("xt", b, kt)
                eng.wait("pad", i, L + 1)
                if b and (b > 1 or kt):
                    eng.wait("f lo", *back(KD, b, kt, 1))
                elif b or kt >= 2:
                    eng.wait("f lo", *back(KD, b, kt, 2))
                eng.do(lambda e, j=j, p=p, q=q, op=op: e.tensor_tensor(buf[:, j, :], d[p], d[q], op), ("filt", b, kt, j))

        def split_x(b, kt):
            buf = v[:, 0, :].rearrange("p (j n) -> p j n", j=FILT) if b == 0 and kt % 2 else filt[:, :, :]
            if b:
                act.wait("conv", b - 1, C_ORDER[-1])
            for j in range(FILT):
                act.wait("filt", b, kt, j)
            act.do(lambda e: e.activation(f_hi[:, kt, :, :], buf, ACT.Copy), ("f hi", b, kt))
            dve.wait("f hi", b, kt)
            dve.do(lambda e: e.tensor_tensor(f_lo[:, kt, :, :], buf, f_hi[:, kt, :, :].bitcast(F32), ALU.subtract),
                   ("f lo", b, kt))

        def back(size, b, i, by):
            return divmod(b * size + i - by, size)

        def conv(b, turn, slot):
            c, j, half = C_ORDER[turn], J_ORDER[slot // HALVES], slot % HALVES
            outer_bank, inner_bank = conv_banks[turn % 2]
            if slot == 0:
                if turn >= 2:
                    pe.wait("conv read", b, turn - 2)
                elif turn == 1:
                    drained("stream")
                elif b:
                    for g in range(2):
                        pe.wait("scores read", b - 1, HP - 1, g)
            acc = outer_bank[:, (j // 3) * L2:(j // 3 + 1) * L2] if j in (0, 3) else inner_bank[:, (j - 1) * L2:j * L2]
            k, wh, wl = use_chunk("conv", b, c, j, half)
            for i in range(HALF):
                kt = half * HALF + i
                pe.wait("f lo", b, kt)
                last = half == HALVES - 1 and i == HALF - 1
                names = [("chunk used", k)] if i == HALF - 1 else []
                names += [("conv", b, c)] if last and slot == SLOTS - 1 else []
                cols = slice(i * P, (i + 1) * P)
                mm3(acc, wh[:, cols], wl[:, cols], f_hi[:, kt, j, :], f_lo[:, kt, j, :], half == 0 and i == 0, last, *names)
            if slot == SLOTS - 1:
                combine(b, turn, c, outer_bank, inner_bank)

        def combine(b, turn, c, outer_bank, inner_bank):
            def out_of_psum():
                act.wait("conv", b, c)
                if turn:
                    act.wait("m12 sums", b, C_ORDER[turn - 1], 1)
                elif b:
                    act.wait("scores", b - 1, HP - 1, 1)
                act.do(lambda e: e.activation(m12, inner_bank[:, :].rearrange("p (j n) -> p j n", j=2), ACT.Copy), ("m12", b, c))
                if turn:
                    pool.wait("conv read", b, turn - 1)
                pool.wait("m12", b, c)
                for i, op in enumerate((ALU.add, ALU.subtract)):
                    pool.do(lambda e, i=i, op=op: e.tensor_tensor(m12_sums[:, i, :], m12[:, 0, :], m12[:, 1, :], op),
                            ("m12 sums", b, c, i))

            def add_up():
                if turn:
                    dve.wait("c", b, C_ORDER[turn - 1])
                elif b:
                    dve.wait("prob turned", b - 1, HP - 1, 1)
                else:
                    dve.wait("lora lo")
                dve.wait("small")
                dve.wait("m12 sums", b, c, 0)
                dve.do(lambda e: e.scalar_tensor_tensor(out=conv_out[:, 0:L:2], in0=outer_bank[:, 0:L2], scalar=conv_bias(c),
                                                        in1=m12_sums[:, 0, :], op0=ALU.add, op1=ALU.add), ("even", b, c))
                dve.wait("m12 sums", b, c, 1)
                dve.do(lambda e: e.scalar_tensor_tensor(out=conv_out[:, 1:L:2], in0=m12_sums[:, 1, :], scalar=conv_bias(c),
                                                        in1=outer_bank[:, L2:L], op0=ALU.add, op1=ALU.subtract), ("conv read", b, turn))

            def split_up():
                if b:
                    act.wait(*(("qk", b - 1, HP - 1) if c < 2 * KW else ("v full", b - 1, 1, TB - 1)))
                act.wait("conv read", b, turn)
                act.do(lambda e: e.activation(c_hi[:, c, :], conv_out, ACT.Copy), ("c hi", b, c))
                dve.wait("c hi", b, c)
                dve.do(lambda e: e.tensor_tensor(c_lo[:, c, :], conv_out, c_hi[:, c, :].bitcast(F32), ALU.subtract), ("c", b, c))

            later(1, out_of_psum)
            later(2, add_up)
            later(3, split_up)

        def split_out(n, acc, hi, lo, bias_col, ready, done):
            act.wait(*ready)
            act.do(lambda e: e.activation(hi, acc, ACT.Identity, bias=bias_col), ("hi of",) + done)
            dve.wait("hi of", *done)
            names = [done] + ([("stream read", n)] if n is not None else [])
            dve.do(lambda e: e.scalar_tensor_tensor(out=lo, in0=acc, scalar=bias_col, in1=hi.bitcast(F32),
                                                    op0=ALU.add, op1=ALU.subtract), *names)

        def project_v(b, n, t):
            if n == 0 and t == 0:
                pe.wait("conv read", b, NC - 2)
            u, acc = take("v")
            toks = slice(t * P, (t + 1) * P)
            for kt in range(KW):
                k, wh, wl = use_chunk("v", b, n, kt)
                c = 2 * KW + kt
                pe.wait("c", b, c)
                names = [("v full", b, n, t)] if kt == KW - 1 else []
                names += [("chunk used", k)] if t == TB - 1 else []
                mm3(acc[:, :], c_hi[:, c, toks], c_lo[:, c, toks], wh[:, :], wl[:, :], kt == 0, kt == KW - 1, *names)
            act.wait("v full", b, n, t)
            if b:
                act.wait("moe out", b - 1, t)
            act.do(lambda e: e.activation(v[:, t, n * 512:(n + 1) * 512], acc[:, :], ACT.Copy),
                   ("v", b, n, t), ("v read", u))

        def project_qk(b, h, j):
            if h == 0:
                pe.wait("conv read", b, NC - 1)
            k, wh, wl = use_chunk("qk", b, h)
            n, acc = take("stream")
            for kt in range(KW):
                c = j * KW + kt
                pe.wait("c", b, c)
                cols = slice((j * KW + kt) * P, (j * KW + kt + 1) * P)
                names = [("qk part", b, h, j)] if kt == KW - 1 else []
                names += [("qk", b, h), ("chunk used", k)] if kt == KW - 1 and j == 1 else []
                mm3(acc[:, :], wh[:, cols], wl[:, cols], c_hi[:, c, :], c_lo[:, c, :], kt == 0, kt == KW - 1, *names)
            eng = dve if j else act
            eng.wait("qk part", b, h, j)
            if h:
                eng.wait("scores", b, h - 1, 1)
            if j:
                dve.do(lambda e: e.tensor_scalar(k_t[:, :], acc[:, :], head_bias(1, h), None, ALU.add),
                       ("qk sb", b, h, 1), ("stream read", n))
            else:
                act.do(lambda e: e.activation(q_t[:, :], acc[:, :], ACT.Identity, bias=head_bias(0, h)),
                       ("qk sb", b, h, 0), ("stream read", n))

        def scores(b, h):
            if h == 0:
                drained("v")
            for g in range(2):
                rows = slice(g * DH, (g + 1) * DH)
                pe.wait("qk sb", b, h, 0)
                pe.wait("qk sb", b, h, 1)
                if h:
                    pe.wait("scores read", b, h - 1, g)
                for t in range(TB):
                    toks = slice(t * P, (t + 1) * P)
                    mm(score_banks[g][:, toks], q_t[rows, toks], k_t[rows, toks], True, True,
                       *([("scores", b, h, g)] if t == TB - 1 else []))
            for g in range(2):
                dve.wait("scores", b, h, g)
                if h:
                    dve.wait("prob turned", b, h - 1, g)
                for t in range(TB):
                    dve.do(lambda e, g=g, t=t: e.tensor_tensor_reduce(
                        prob[:, g, t, :], score_banks[g][:, t * P:(t + 1) * P], mask[:, :], 1.0, NEG_INF * 4,
                        ALU.add, ALU.max, top[:, g, t:t + 1]), *([("scores read", b, h, g)] if t == TB - 1 else []))
                dve.wait("scores read", b, h, g)
                dve.do(lambda e, g=g: e.tensor_scalar(ntop[:, g, :], top[:, g, :], -QK_SCALE, None, ALU.mult),
                       ("ntop", b, h, g))

        def probabilities(b, h, g):
            act.wait("ntop", b, h, g)
            for t in range(TB):
                act.do(lambda e, t=t: e.activation(prob[:, g, t, :], prob[:, g, t, :], ACT.Exp,
                                                   bias=ntop[:, g, t:t + 1], scale=QK_SCALE,
                                                   accum_out=total[:, g, t:t + 1]),
                       *([("exp", b, h, g)] if t == TB - 1 else []))
            dve.wait("exp", b, h, g)
            dve.do(lambda e: e.reciprocal(rtotal[:, g, :], total[:, g, :]), ("rtotal", b, h, g))
            pool.wait("rtotal", b, h, g)
            pool.do(lambda e: e.tensor_tensor(
                prob[:, g, :, :], prob[:, g, :, :],
                rtotal[:, g, :].rearrange("p (t o) -> p t o", o=1).broadcast_to([P, TB, P]), ALU.mult),
                ("prob", b, h, g))

        def turn_prob(b, h):
            for g in range(2):
                n, dst = take("turn")
                pe.wait("prob", b, h, g)
                for t in range(TB):
                    pe.do(lambda e, g=g, t=t, dst=dst: e.transpose(dst[:, t * P:(t + 1) * P], prob[:, g, t, :], ident[:, :]),
                          *([("prob turned", b, h, g)] if t == TB - 1 else []))
                dve.wait("prob turned", b, h, g)
                if h:
                    dve.wait("pv part", b, h - 1, g)
                dve.do(lambda e, g=g, dst=dst: e.tensor_copy(prob_t[:, g, :], dst[:, :]), ("prob t", b, h, g), ("turn read", n))

        def attend(b, h):
            n, acc = take("stream")
            for g in range(2):
                pe.wait("prob t", b, h, g)
                for t in range(TB):
                    pe.wait("v", b, (2 * h + g) * DH // 512, t)
                    names = [("pv part", b, h, g)] if t == TB - 1 else []
                    names += [("pv", b, h)] if t == TB - 1 and g == 1 else []
                    head = (2 * h + g) * DH
                    mm(acc[g * DH:(g + 1) * DH, t * P:(t + 1) * P], v[:, t, head:head + DH],
                       prob_t[:, g, t * P:(t + 1) * P], True, True, *names)
            if h:
                act.wait("wo", b, h - 1)
            split_out(n, acc[:, :], o_hi[:, :], o_lo[:, :], head_bias(2, h), ("pv", b, h), ("o", b, h))

        def project_wo(b, h):
            if h == 0:
                drained("side")
            k, wh, wl = use_chunk("wo", b, h)
            pe.wait("o", b, h)
            for m in range(KW):
                cols = slice(m * P, (m + 1) * P)
                names = [("wo", b, h), ("chunk used", k)] if m == KW - 1 else []
                mm3(wo_banks[m][:, :], wh[:, cols], wl[:, cols], o_hi[:, :], o_lo[:, :], h == 0, h == HP - 1, *names)

        def finish_wo(b):
            for m in range(KW):
                split_out(None, wo_banks[m][:, :], po_hi[:, m, :], po_lo[:, m, :], out_bias(m),
                          ("wo", b, HP - 1), ("po", b, m))

        def load_residual(b, t):
            if b + 1 < NB:
                sp.wait("x turned", b + 1, KD - 1)
            sp.dma(work[t][:, :], x[b * TB + t], s_work[t], counts, ("residual", b, t))

        def project_out(b, t0, n):
            for t in (t0, t0 + 1):
                u, acc = take("side")
                toks = slice(t * P, (t + 1) * P)
                for kt in range(KW):
                    k, wh, wl = use_chunk("proj", b, t0, n, kt)
                    pe.wait("po", b, kt)
                    names = [("proj", b, t, n)] if kt == KW - 1 else []
                    names += [("chunk used", k)] if t == t0 + 1 else []
                    mm3(acc[:, :], po_hi[:, kt, toks], po_lo[:, kt, toks], wh[:, :], wl[:, :], kt == 0, kt == KW - 1, *names)
                add_proj_bias(b, t, n, u, acc)

        def add_proj_bias(b, t, n, u, acc):
            dve.wait("proj", b, t, n)
            dve.wait("pv", b, HP - 1)
            half = y[t][:, n * 512:(n + 1) * 512]
            dve.do(lambda e: e.tensor_tensor(half, acc[:, :], projb[:, n * 512:(n + 1) * 512], ALU.add),
                   ("attn out", b, t, n), ("side read", u))
            dve.wait("attn out", b, t, n)
            dve.do(lambda e: e.bn_stats(stats[:, t, n, :], half), ("stats", "ln2", b, t, n))

        def add_norm2(b, t0):
            inverse_std("ln2", b, t0, PR)

            def add_up():
                for t in (t0, t0 + 1):
                    scale_row("ln2", b, t0, t, y[t], y[t], ("ln2", b, t))
                    pool.wait("residual", b, t)
                    pool.wait("ln2", b, t)
                    pool.do(lambda e, t=t: e.tensor_tensor(work[t][:, :], work[t][:, :], y[t], ALU.add), ("x1", b, t))
            later(1, add_up)

        def norm3(b, t0):
            for t in (t0, t0 + 1):
                dve.wait("x1", b, t)
                row_stats("ln3", b, t, [work[t][:, 0:512], work[t][:, 512:1024]])
            inverse_std("ln3", b, t0, PR)

            def scale():
                for t in (t0, t0 + 1):
                    scale_row("ln3", b, t0, t, y[t], work[t][:, :], ("ln3", b, t))
            later(3, scale)

        def lora_mid(b, t):
            pe.wait("ln3", b, t)
            for half in range(2):
                n, dst = take("turn")
                for i in range(4):
                    kt = half * 4 + i
                    pe.do(lambda e, i=i, kt=kt, dst=dst: e.transpose(dst[:, i * P:(i + 1) * P], y[t][:, kt * P:(kt + 1) * P], ident[:, :]),
                          *([("x3 turned", b, t, half)] if i == 3 else []))
                act.wait("x3 turned", b, t, half)
                if t:
                    act.wait("mid", b, t - 1)
                act.do(lambda e, half=half, dst=dst: e.activation(x3_t[:, half * 4:(half + 1) * 4, :],
                                                                  dst[:, :].rearrange("p (k n) -> p k n", n=P), ACT.Copy),
                       ("x3_t", b, t, half), ("turn read", n))

        def back_pair(b, t):
            n, i = back(TB // PR, b, t // PR, 1)
            return n, i * PR

        def lora_mid2(b, t):
            i = t % PR
            n, acc = take("side")
            for kt in range(KD):
                pe.wait("x3_t", b, t, kt // 4)
                mm(acc[:, 0:ER + E], x3_t[:, kt, :], aw_sb[:, kt, :], kt == 0, kt == KD - 1,
                   *([("mid", b, t)] if kt == KD - 1 else []))

            def out_of_psum():
                dve.wait("mid", b, t)
                if (b, t) >= (0, PR):
                    dve.wait("mid2", *back_pair(b, t))
                dve.do(lambda e: e.tensor_copy(mid[:, i, :], acc[:, 0:ER]))
                dve.do(lambda e: e.tensor_copy(logits[:, i, :], acc[:, ER:ER + E]), ("logits", b, t), ("side read", n))
            later(1, out_of_psum)

        def gates(b, t0):
            wide = [P, PR, E, E]
            own = logits[:, :, :].rearrange("p t (i o) -> p t i o", o=1).broadcast_to(wide)
            other = logits[:, :, :].rearrange("p t (o j) -> p t o j", o=1).broadcast_to(wide)
            spread = lambda a, n: a[:, :].rearrange("p (t o) -> p t o", o=1).broadcast_to([P, PR, n])
            dve.wait("logits", b, t0 + 1)
            link(lambda e: e.tensor_reduce(gtop[:, :], logits[:, :, :], AX.X, ALU.max))
            dve.do(lambda e: e.tensor_tensor(gexp[:, :, :], logits[:, :, :], spread(gtop, E), ALU.subtract), ("shifted", b, t0))
            act.wait("shifted", b, t0)
            act.do(lambda e: e.activation(gexp[:, :, :], gexp[:, :, :], ACT.Exp), ("gexp", b, t0))
            dve.do(lambda e: e.tensor_tensor(above[:, :, :, :], other, own, ALU.is_gt))
            link(lambda e: e.tensor_tensor(tied[:, :, :, :], other, own, ALU.is_equal))
            link(lambda e: e.tensor_tensor(tied[:, :, :, :], tied[:, :, :, :], before[:, :, :, :], ALU.mult))
            link(lambda e: e.tensor_tensor(above[:, :, :, :], above[:, :, :, :], tied[:, :, :, :], ALU.add))
            link(lambda e: e.tensor_reduce(rank[:, :, :], above[:, :, :, :], AX.X, ALU.add))
            dve.wait("gexp", b, t0)
            link(lambda e: e.scalar_tensor_tensor(out=gate[:, :, :], in0=rank[:, :, :], scalar=float(TOP_K), in1=gexp[:, :, :],
                                                  op0=ALU.is_lt, op1=ALU.mult))
            link(lambda e: e.tensor_reduce(gsum[:, :], gate[:, :, :], AX.X, ALU.add))
            link(lambda e: e.reciprocal(gsum[:, :], gsum[:, :]))
            link(lambda e: e.scalar_tensor_tensor(out=gate[:, :, :], in0=gate[:, :, :], scalar=LORA_SCALE, in1=spread(gsum, E),
                                                  op0=ALU.mult, op1=ALU.mult))
            by_expert = mid[:, :, :].rearrange("p t (e r) -> p t e r", r=R)
            link(lambda e: e.tensor_tensor(by_expert, by_expert, gate[:, :, :].rearrange("p t (e o) -> p t e o", o=1)
                                           .broadcast_to([P, PR, E, R]), ALU.mult))
            link(lambda e: e.tensor_copy(mid2[:, :, 0:ER], mid[:, :, :]))
            dve.do(lambda e: e.tensor_tensor(mid2[:, :, ER:2 * ER], mid[:, :, :], mid2[:, :, 0:ER].bitcast(F32), ALU.subtract),
                   ("mid2", b, t0))

        def turn_mid(b, t0):
            n, dst = take("turn")
            pe.wait("mid2", b, t0)
            for i in range(PR):
                pe.do(lambda e, i=i: e.transpose(dst[:, i * P:(i + 1) * P], mid2[:, i, :].bitcast(F32), ident[:, :]),
                      *([("mid turned", b, t0)] if i == PR - 1 else []))
            act.wait("mid turned", b, t0)
            act.do(lambda e: e.activation(mid_t[:, :, :], dst[:, 0:PR * P].rearrange("p (t n) -> p t n", n=P), ACT.Copy),
                   ("mid_t", b, t0), ("turn read", n))

        def lora_out(b, t):
            pe.wait("mid_t", b, t - t % PR)
            pe.wait("lora lo")
            accs = []
            for j in range(2):
                u, acc = take("side")
                accs.append((u, acc))
                cols = slice(j * 512, (j + 1) * 512)
                mm(acc[:, :], mid_t[:, t % PR, :], lora_b[0][:, cols], True, False)
                mm(acc[:, :], mid_t[:, t % PR, :], lora_b[1][:, cols], False, True, ("delta", b, t, j))

            def measure():
                for j, (u, acc) in enumerate(accs):
                    dve.wait("delta", b, t, j)
                    dve.do(lambda e, j=j, acc=acc: e.bn_stats(stats[:, t, j, :], acc[:, :]), ("stats", "ln4", b, t, j))
                inverse_std("ln4", b, t, 1)

            def scale():
                for j, (u, acc) in enumerate(accs):
                    scale_row("ln4", b, t, t, y[t][:, j * 512:(j + 1) * 512], acc[:, :], ("ln4", b, t, j), ("side read", u))
                pool.wait("ln4", b, t, 1)
                pool.do(lambda e: e.tensor_tensor(work[t][:, :], work[t][:, :], y[t], ALU.add), ("moe out", b, t))
                later(2, store)

            def store():
                sp.wait("moe out", b, t)
                sp.dma(out[b * TB + t], work[t][:, :], s_out[t], counts, ("stored", b, t))

            measure()
            later(2, scale)

        SIDE = [
            (9, project_out, 0, 0), (10, project_out, 0, 1), (11, add_norm2, 0),
            (12, project_out, 2, 0), (13, project_out, 2, 1), (14, add_norm2, 2),
            (16, norm3, 0), (19, norm3, 2),
            (21, lora_mid, 0), (22, lora_mid2, 0), (23, lora_mid, 1), (24, lora_mid2, 1),
            (25, lora_mid, 2), (26, gates, 0), (27, lora_mid2, 2), (28, lora_mid, 3), (29, turn_mid, 0), (30, lora_mid2, 3),
            (31, lora_out, 0), (32, gates, 2), (34, lora_out, 1), (35, turn_mid, 2),
            (37, lora_out, 2), (40, lora_out, 3),
            (37, next_x, 0), (40, next_x, 1), (43, next_x, 2), (46, next_x, 3),
        ]

        def side(b):
            plan = {}
            for s, f, *args in SIDE:
                plan.setdefault(s, []).append((f, (b, *args)))
            return plan

        FILL = {HP: 3, HP + 1: 2, HP + 2: 3}
        ALL = NC * SLOTS

        def chunk_order():
            names = []

            def conv_names(b, a, z):
                for s in range(a, z):
                    names.append(("conv", b, C_ORDER[s // SLOTS], J_ORDER[s % SLOTS // HALVES], s % HALVES))
                    for f, args in (side(b - 1) if b else {}).get(s, []):
                        if f is project_out:
                            names.extend(("proj",) + args + (kt,) for kt in range(KW))

            done = 0
            for b in range(NB):
                conv_names(b, done, ALL)
                done = 0
                names.extend(("v", b, n, kt) for n in range(2) for kt in range(KW))
                for i in range(HP + LAG):
                    if i >= LAG:
                        names.append(("wo", b, i - LAG))
                    if i < HP:
                        names.append(("qk", b, i))
                    if b + 1 < NB and i in FILL:
                        conv_names(b + 1, done, done + FILL[i])
                        done += FILL[i]
            names.extend(("proj", NB - 1, t0, n, kt) for t0 in (0, 2) for n in range(2) for kt in range(KW))
            return names

        def conv_chunks(b, a, z):
            plan = side(b - 1) if b else {}
            for s in range(a, z):
                tick()
                conv(b, s // SLOTS, s % SLOTS)
                for f, args in plan.get(s, []):
                    f(*args)

        order = chunk_order()
        plan_chunks(order)
        number.update((name, k) for k, name in enumerate(order))
        for t in range(TB):
            load_x(0, t)
        constants()
        load_chunks()
        setup()
        ln1(0)
        act.wait("small")
        for kt in range(KD):
            turn_x(0, kt)
            if kt:
                split_x(0, kt - 1)
            if kt == 0:
                split_chunks(1)
        split_x(0, KD - 1)
        lora_weights()
        dve.wait("small")
        dve.wait("mask")
        dve.wait("before", E - 1)
        pe.wait("small")
        for t in range(TB):
            sp.wait("x turned", 0, KD - 1)
            load_x(1, t)

        done = 0
        for b in range(NB):
            conv_chunks(b, done, ALL)
            done = 0
            for n in range(2):
                for t in range(TB):
                    tick()
                    project_v(b, n, t)
                if n == 0 and b + 1 < NB:
                    ln1(b + 1)
            settle()
            for i in range(HP + LAG):
                if 2 <= i < HP + 2:
                    turn_prob(b, i - 2)
                if 1 <= i <= HP and b + 1 < NB:
                    split_x(b + 1, i - 1)
                if i >= LAG:
                    project_wo(b, i - LAG)
                if 1 <= i <= HP:
                    scores(b, i - 1)
                    probabilities(b, i - 1, 0)
                if i < HP:
                    project_qk(b, i, 0)
                if 1 <= i <= HP:
                    probabilities(b, i - 1, 1)
                if i < HP:
                    project_qk(b, i, 1)
                if 2 <= i < HP + 2:
                    attend(b, i - 2)
                if i < HP and b + 1 < NB:
                    turn_x(b + 1, i)
                if b + 1 < NB and i in FILL:
                    conv_chunks(b + 1, done, done + FILL[i])
                    done += FILL[i]
            finish_wo(b)
            for t in range(TB):
                load_residual(b, t)
        b = NB - 1
        for t0 in (0, 2):
            project_out(b, t0, 0)
            project_out(b, t0, 1)
            add_norm2(b, t0)
            settle()
        for t0 in (0, 2):
            norm3(b, t0)
            settle()
            for t in (t0, t0 + 1):
                lora_mid(b, t)
                lora_mid2(b, t)
            settle()
            gates(b, t0)
            turn_mid(b, t0)
            for t in (t0, t0 + 1):
                lora_out(b, t)
                settle()
        for t in range(TB):
            sp.wait("stored", b, t)

        with nc.Block() as block:
            block.tensor(pe.emit)
            block.scalar(act.emit)
            block.vector(dve.emit)
            block.gpsimd(pool.emit)
            block.sync(sp.emit)


def kernel(**inputs):
    import numpy as np
    import concourse.bacc as bacc
    from concourse.bass_utils import run_bass_kernel_spmd

    g = {k.replace("L0_attn_", "").replace("L0_ffn_", ""): np.asarray(a) for k, a in inputs.items()}
    flat = lambda a, *s: np.ascontiguousarray(a.reshape(*s))
    columns = lambda a: a.reshape(-1, P).T
    arrays = {
        "x": flat(g["inputs"], NB * TB, P, D),
        "conv_w": flat(g["conv_w"], TAPS, D, 3 * W),
        "wq": flat(g["wq"], W, H * DH),
        "wk": flat(g["wk"], W, H * DH),
        "wv": flat(g["wv"], W, H * DH),
        "wo": flat(g["wo"], H * DH, W),
        "proj_w": flat(g["proj_w"], W, D),
        "biases": np.ascontiguousarray(np.concatenate([columns(g[n]) for n in ("conv_b", "bq", "bk", "bv", "bo")], axis=1)),
        "proj_b": np.ascontiguousarray(np.broadcast_to(g["proj_b"], (P, D))),
        "aw": np.ascontiguousarray(np.concatenate([g["A"].reshape(ER, D).T, g["Wr"].T], axis=1)),
        "b_t": np.ascontiguousarray(g["B"].transpose(0, 2, 1).reshape(ER, D)),
    }
    nc = bacc.Bacc("TRN2", target_bir_lowering=False, num_devices=1)
    aps = {n: nc.dram_tensor(n, a.shape, mybir.dt.from_np(a.dtype), kind="ExternalInput").ap() for n, a in arrays.items()}
    out = nc.dram_tensor("out", (NB * TB, P, D), F32, kind="ExternalOutput").ap()
    build(nc, out=out, **aps)
    result = run_bass_kernel_spmd(nc, [arrays], core_ids=[0]).results[0]["out"]
    return result.reshape(NB, L, D)
```

```python
import concourse.bass as bass
from concourse import mybir
from contextlib import ExitStack

F32 = mybir.dt.float32
I32 = mybir.dt.int32
F32R = mybir.dt.float32r
ALU = mybir.AluOpType
ACT = mybir.ActivationFunctionType
AX = mybir.AxisListType

P = 128
NB, L, D = 4, 512, 1024
TB = L // P
KD = D // P
W = 256
KW = W // P
NC = 3 * KW
C_ORDER = [4, 5, 0, 1, 2, 3]
TAPS = 3
FILT = 4
J_ORDER = [0, 3, 1, 2]
L2 = L // 2
H, DH = 16, 64
HP = H // 2
E, R = 4, 16
ER = E * R
LORA_SCALE = 16.0 / 16.0 ** 0.5
TOP_K = 2
EPS = 1e-5
GUESS = float(0x5F3759DF - 2 ** 31 - 2 ** 22)
NEWTON_STEPS = 3
QK_SCALE = 1.0 / DH ** 0.5
NEG_INF = -1e9 / QK_SCALE
CHUNK = 512
HALF = CHUNK // P
HALVES = KD // HALF
SLOTS = FILT * HALVES
RAW_SLOTS, SPLIT_SLOTS = 6, 6
SUM_LEAD = 1
LOW_ON_DVE = {5, 7, 10, 11, 16, 22, 23, 24, 25, 26, 31, 32, 33, 38, 42, 45, 46, 47}
LOW_ON_DVE_FIRST = {1, 2, 5, 8, 11, 12, 15, 19, 20, 21, 23, 25, 29, 35, 36, 37, 40, 42, 46, 47}
LEAD = 5
NORM3_LAG, OUT_LAG, STORE_LAG = 1, 4, 1
LAG = 3


class Queue:

    def __init__(self, sem, where):
        self.sem, self.where, self.items, self.count = sem, where, [], 0

    def wait(self, *name):
        assert name in self.where, name
        self.items.append(("wait", name))

    def do(self, ins, *names):
        if names:
            self.count += 1
            for n in names:
                assert n not in self.where, n
                self.where[n] = (self.sem, self.count)
        self.items.append(("do", ins, self.sem if names else None, 1))

    def dma(self, out, in_, sem, counts, *names):
        counts[sem.name] = counts.get(sem.name, 0) + 16
        for n in names:
            self.where[n] = (sem, counts[sem.name])
        self.items.append(("do", lambda e: e.dma_start(out, in_), sem, 16))

    def emit(self, eng):
        seen = {}
        for item in self.items:
            if item[0] == "wait":
                sem, value = self.where[item[1]]
                if seen.get(sem.name, 0) < value:
                    eng.wait_ge(sem, value)
                    seen[sem.name] = value
            else:
                ins = item[1](eng)
                if item[2] is not None:
                    ins.then_inc(item[2], item[3])


def build(nc, x, conv_w, wq, wk, wv, wo, proj_w, biases, proj_b, aw, b_t, out):
    with ExitStack() as ctx:
        def sb(name, shape, dt=F32):
            return ctx.enter_context(nc.sbuf_tensor(name, shape, dt))

        def sem(name):
            return ctx.enter_context(nc.semaphore(name))

        ident = sb("ident", [P, P])
        mask = sb("mask", [P, P])
        bias = sb("bias", [P, NC + 3 * HP + KW])
        conv_bias = lambda c: bias[:, c:c + 1]
        head_bias = lambda j, h: bias[:, NC + j * HP + h:NC + j * HP + h + 1]
        out_bias = lambda m: bias[:, NC + 3 * HP + m:NC + 3 * HP + m + 1]
        projb = sb("projb", [P, D])
        aw_sb = sb("aw_sb", [P, KD, ER + E])
        lora_b = [sb(f"lora_b{i}", [P, D], F32R) for i in range(2)]
        raw_slots = [sb(f"raw{i}", [P, CHUNK]) for i in range(RAW_SLOTS)]
        w_hi = [sb(f"w_hi{i}", [P, CHUNK], F32R) for i in range(SPLIT_SLOTS)]
        w_lo = [sb(f"w_lo{i}", [P, CHUNK], F32R) for i in range(SPLIT_SLOTS)]
        xt = [sb(f"xt{i}", [P, L + 2]) for i in range(2)]
        filt = sb("filt", [P, FILT, L2])
        f_hi = sb("f_hi", [P, KD, FILT, L2], F32R)
        f_lo = sb("f_lo", [P, KD, FILT, L2], F32R)
        c_hi = sb("c_hi", [P, NC, L], F32R)
        c_lo = sb("c_lo", [P, NC, L], F32R)
        q_t = sb("q_t", [P, L])
        k_t = sb("k_t", [P, L])
        v = sb("v", [P, TB, H * DH])
        prob = sb("prob", [P, 2, TB, P])
        prob_t = sb("prob_t", [P, 2, TB * P])
        top = sb("top", [P, 2, TB])
        ntop = sb("ntop", [P, 2, TB])
        total = sb("total", [P, 2, TB])
        rtotal = sb("rtotal", [P, 2, TB])
        o_hi = sb("o_hi", [P, L], F32R)
        o_lo = sb("o_lo", [P, L], F32R)
        po_hi = sb("po_hi", [P, KW, L], F32R)
        po_lo = sb("po_lo", [P, KW, L], F32R)
        work = [sb(f"work{t}", [P, D]) for t in range(TB)]
        y = [v[:, t, :] for t in range(TB)]
        x3_t = prob_t[:, :, :].rearrange("p g (k n) -> p (g k) n", n=P)
        m12 = q_t[:, :].rearrange("p (j n) -> p j n", j=2)
        m12_sums = k_t[:, :].rearrange("p (j n) -> p j n", j=2)
        conv_out = prob[:, 0, :, :].rearrange("p t n -> p (t n)")
        tap1, outer, inner = v[:, 1, :], v[:, 2, :], v[:, 3, :]
        sums = [prob_t[:, 0, :], prob_t[:, 1, :], prob[:, 1, :, :].rearrange("p t n -> p (t n)")]
        lora_raw = [q_t, k_t]
        norms = {}
        for name in ("ln1", "ln2", "ln3", "ln4"):
            norms[name] = (sb(name + "_mv", [P, TB, 2]), sb(name + "_r", [P, TB]), sb(name + "_nmr", [P, TB]))
        stats = sb("stats", [P, TB, 2, nc.vector.BN_STATS_DIM])
        varh = sb("varh", [P, TB])
        newton = sb("newton", [P, TB])
        PR = 2
        logits = sb("logits", [P, PR, E])
        above = sb("above", [P, PR, E, E])
        tied = sb("tied", [P, PR, E, E])
        before = sb("before", [P, PR, E, E])
        rank = sb("rank", [P, PR, E])
        gtop = sb("gtop", [P, PR])
        gexp = sb("gexp", [P, PR, E])
        gate = sb("gate", [P, PR, E])
        gsum = sb("gsum", [P, PR])
        mid = sb("mid", [P, PR, ER])
        mid2 = sb("mid2", [P, PR, 2 * ER], F32R)
        mid_t = sb("mid_t", [P, PR, P], F32R)
        bank = [ctx.enter_context(nc.psum_tensor(f"bank{i}", [P, 512], F32)) for i in range(8)]
        score_banks, wo_banks = bank[2:4], bank[6:8]
        conv_banks = [bank[2:4], bank[0:2]]
        banks_of = {
            "stream": bank[0:2],
            "v": bank[2:4],
            "turn": bank[4:6],
            "side": bank[6:8],
        }

        where, counts = {}, {}
        pe = Queue(sem("pe_steps"), where)
        act = Queue(sem("act_steps"), where)
        dve = Queue(sem("dve_steps"), where)
        pool = Queue(sem("pool_steps"), where)
        sp = Queue(sem("sp_steps"), where)
        s_raw = [sem(f"s_raw{i}") for i in range(RAW_SLOTS)]
        s_store = [sem(f"s_store{i}") for i in range(len(sums))]
        s_work = [sem(f"s_work{t}") for t in range(TB)]
        s_out = [sem(f"s_out{t}") for t in range(TB)]
        s_tap1 = [sem(f"s_tap1_{h}") for h in range(HALVES)]
        s_small = sem("s_small")
        s_lora = sem("s_lora")
        links = [0]

        def link(ins):
            links[0] += 1
            dve.do(ins, ("dve link", links[0]))
            dve.wait("dve link", links[0])

        def mm(dst, lhs, rhs, start, stop, *names):
            pe.do(lambda e: e.matmul(dst, lhs, rhs, start=start, stop=stop), *names)

        def mm3(dst, w_h, w_l, m_h, m_l, start, stop, *names):
            mm(dst, w_h, m_h, start, False)
            mm(dst, w_h, m_l, False, False)
            mm(dst, w_l, m_h, False, stop, *names)

        uses = dict.fromkeys(banks_of, 0)

        def take(kind):
            n = uses[kind]
            uses[kind] = n + 1
            if n >= 2:
                pe.wait(kind + " read", n - 2)
            return n, banks_of[kind][n % 2]

        def drained(kind):
            for n in range(max(uses[kind] - 2, 0), uses[kind]):
                pe.wait(kind + " read", n)

        summed = nc.dram_tensor("summed_filters", (NC, 2, HALVES, P, CHUNK), F32, kind="Internal").ap()

        def tap_half(tap, c, half):
            rows = slice(half * HALF * P, (half + 1) * HALF * P)
            return conv_w[tap, rows, c * P:(c + 1) * P].rearrange("(k p) n -> p k n", p=P)

        chunks = []

        def conv_chunk(b, c, j, half):
            if j == 0:
                parts = [(0, tap_half(0, c, half))]
            elif j == 3:
                parts = [(0, tap_half(2, c, half))]
            else:
                parts = [(0, summed[c, j - 1, half].rearrange("p (k n) -> p k n", k=HALF))] if b else []
            return ("conv", b, c, j, half), CHUNK, parts

        def columns_of(w, at, n):
            return w[:, at:at + n].rearrange("(k p) n -> p k n", p=P)

        def row_tile(w, kt, at, n):
            return w[kt * P:(kt + 1) * P, at:at + n].rearrange("p (k n) -> p k n", k=1)

        def plan_chunks(order):
            for name in order:
                kind, b = name[0], name[1]
                if kind == "conv":
                    chunks.append(conv_chunk(*name[1:]))
                elif kind == "v":
                    chunks.append((name, CHUNK, [(0, row_tile(wv, name[3], name[2] * 512, 512))]))
                elif kind == "proj":
                    chunks.append((name, CHUNK, [(0, row_tile(proj_w, name[4], name[3] * 512, 512))]))
                elif kind == "qk":
                    chunks.append((name, CHUNK, [(j * KW * P, columns_of(w, name[2] * P, P)) for j, w in enumerate((wq, wk))]))
                elif kind == "wo":
                    chunks.append((name, KW * P, [(0, row_tile(wo, name[2], 0, KW * P))]))

        number = {}
        loaded, split, summed_upto = [0], [0], [0]
        raw, in_raw, summing = {}, [], []

        clock, pending = [0], []

        def later(ticks, step):
            pending.append((clock[0] + ticks, step))

        def tick():
            clock[0] += 1
            due = [p for p in pending if p[0] <= clock[0]]
            pending[:] = [p for p in pending if p[0] > clock[0]]
            for _, step in due:
                step()

        def settle():
            while pending:
                tick()

        def load_chunks():
            while loaded[0] < len(chunks):
                k = loaded[0]
                name, _, parts = chunks[k]
                if parts:
                    n = len(in_raw)
                    last = in_raw[n - RAW_SLOTS] if n >= RAW_SLOTS else None
                    if last is not None and ("split lo", last) not in where:
                        break
                    if name[:2] == ("conv", 0) and name[3:] == (0, 0) and not tap1_free(name[2]):
                        break
                    if last is not None:
                        sp.wait("split hi", last)
                        sp.wait("split lo", last)
                        if chunks[last][0][:2] == ("conv", 0):
                            sp.wait("kept", last)
                    in_raw.append(k)
                    if name[0] == "conv" and name[1] == 1 and name[3] in (1, 2):
                        sp.wait("kept", number["conv", 0, *name[2:]])
                    slot = raw[k] = raw_slots[n % RAW_SLOTS]
                    for at, src in parts:
                        kt, cols = src.shape[1], src.shape[2]
                        sp.dma(slot[:, at:at + kt * cols].rearrange("p (k n) -> p k n", k=kt), src,
                               s_raw[n % RAW_SLOTS], counts, ("raw", k))
                loaded[0] += 1
                if name[:2] == ("conv", 0) and name[3:] == (0, 0):
                    load_tap1(name[2])

        def tap1_free(c):
            return c == C_ORDER[0] or ("inner", C_ORDER[C_ORDER.index(c) - 1], HALVES - 1) in where

        def load_tap1(c):
            if c != C_ORDER[0]:
                sp.wait("inner", C_ORDER[C_ORDER.index(c) - 1], HALVES - 1)
            for h in range(HALVES):
                sp.dma(tap1[:, h * CHUNK:(h + 1) * CHUNK].rearrange("p (k n) -> p k n", k=HALF), tap_half(1, c, h),
                       s_tap1[h], counts, ("tap1", c, h))

        def sum_filters(k, c, j, half):
            cols = slice(half * CHUNK, (half + 1) * CHUNK)
            if j == 0:
                dve.wait("raw", k)
                if summing:
                    dve.wait("raw", summing[-1])
                dve.do(lambda e: e.tensor_copy(outer[:, cols], raw[k][:, :]), ("kept", k))
            elif j == 3:
                dve.wait("raw", k)
                dve.wait("kept", number["conv", 0, c, 0, half])
                dve.do(lambda e: e.tensor_tensor(outer[:, cols], outer[:, cols], raw[k][:, :], ALU.add), ("outer", c, half), ("kept", k))
                dve.wait("tap1", c, half)
                dve.do(lambda e: e.tensor_scalar(inner[:, cols], tap1[:, cols], 0.5, None, ALU.mult), ("inner", c, half))
            else:
                s = len(summing)
                summing.append(k)
                dst = sums[s % len(sums)]
                raw[k] = dst
                if s >= len(sums):
                    for reader in ("kept", "split hi", "split lo"):
                        dve.wait(reader, summing[s - len(sums)])
                dve.wait("outer", c, half)
                dve.wait("inner", c, half)
                dve.do(lambda e: e.scalar_tensor_tensor(out=dst, in0=outer[:, cols], scalar=0.5, in1=inner[:, cols],
                                                        op0=ALU.mult, op1=ALU.add if j == 1 else ALU.subtract), ("raw", k))
                sp.wait("raw", k)
                sp.dma(summed[c, j - 1, half], dst, s_store[s % len(sums)], counts, ("kept", k))

        def on_dve(name):
            if name[0] != "conv":
                return False
            _, b, c, j, half = name
            turn = C_ORDER.index(c)
            at = turn * SLOTS + order_of(b, turn).index((j, half))
            return at in (LOW_ON_DVE if b else LOW_ON_DVE_FIRST)

        def split_chunks(upto):
            load_chunks()
            while summed_upto[0] <= min(upto + SUM_LEAD, len(chunks) - 1):
                k = summed_upto[0]
                summed_upto[0] += 1
                if chunks[k][0][:2] == ("conv", 0):
                    sum_filters(k, *chunks[k][0][2:])
            while split[0] <= min(upto, len(chunks) - 1):
                k = split[0]
                if k >= SPLIT_SLOTS and ("chunk used", k - SPLIT_SLOTS) not in where:
                    break
                split[0] += 1
                name, n, _ = chunks[k]
                src, hi, lo = raw[k][:, 0:n], w_hi[k % SPLIT_SLOTS][:, 0:n], w_lo[k % SPLIT_SLOTS][:, 0:n]
                if k >= SPLIT_SLOTS:
                    act.wait("chunk used", k - SPLIT_SLOTS)
                low = dve if on_dve(name) else pool
                act.wait("raw", k)
                act.do(lambda e, hi=hi, src=src: e.activation(hi, src, ACT.Copy), ("split hi", k))
                low.wait("split hi", k)
                low.do(lambda e, lo=lo, hi=hi, src=src: e.tensor_tensor(lo, src, hi.bitcast(F32), ALU.subtract), ("split lo", k))
                load_chunks()

        def use_chunk(*name):
            k = number[name]
            split_chunks(k + LEAD)
            pe.wait("split hi", k)
            pe.wait("split lo", k)
            return k, w_hi[k % SPLIT_SLOTS], w_lo[k % SPLIT_SLOTS]

        def setup():
            sp.dma(bias[:, :], biases, s_small, counts)
            sp.dma(projb[:, :], proj_b, s_small, counts)
            sp.dma(aw_sb[:, :, :], aw.rearrange("(k p) n -> p k n", p=P), s_small, counts, ("small",))
            for rows in (slice(0, ER), slice(ER, 2 * ER)):
                for i, half in enumerate(lora_raw):
                    sp.dma(half[rows, :], b_t[:, i * 512:(i + 1) * 512], s_lora, counts, ("lora raw",))

        def constants():
            pool.do(lambda e: e.memset(ident[:, :], 0.0), ("ident zero",))
            pool.do(lambda e: e.memset(mask[:, :], 0.0), ("mask zero",))
            pool.wait("ident zero")
            pool.do(lambda e: e.affine_select(out=ident[:, :], in_=ident[:, :], compare_op=ALU.not_equal, fill=1.0,
                                              base=0, pattern=[[-1, P]], channel_multiplier=1), ("ident",))
            pool.wait("mask zero")
            pool.do(lambda e: e.affine_select(out=mask[:, :], in_=mask[:, :], compare_op=ALU.is_ge, fill=NEG_INF,
                                              base=0, pattern=[[-1, P]], channel_multiplier=1), ("mask",))
            for i in range(2):
                for col in (0, L + 1):
                    pool.do(lambda e, i=i, col=col: e.memset(xt[i][:, col:col + 1], 0.0), ("pad", i, col))
            pool.do(lambda e: e.memset(before[:, :, :, :], 0.0), ("before zero",))
            pool.wait("before zero")
            for i in range(1, E):
                pool.do(lambda e, i=i: e.memset(before[:, :, i, 0:i], 1.0), ("before", i))

        def lora_weights():
            act.wait("lora raw")
            for i, src in enumerate(lora_raw):
                hi, lo = (w[:, i * 512:(i + 1) * 512] for w in lora_b)
                act.do(lambda e, src=src, hi=hi: e.activation(hi, src[:, :], ACT.Copy), ("lora hi", i))
                dve.wait("lora hi", i)
                dve.do(lambda e, src=src, hi=hi, lo=lo: e.tensor_tensor(lo, src[:, :], hi.bitcast(F32), ALU.subtract), ("lora lo", i))

        def inverse_std(norm, b, t0, n):
            mv, rr, nmr = norms[norm]
            ts = slice(t0, t0 + n)
            for t in range(t0, t0 + n):
                for half in range(2):
                    dve.wait("stats", norm, b, t, half)
            for t in range(t0, t0 + n):
                (link if t == t0 + n - 1 else dve.do)(lambda e, t=t: e.bn_aggr(mv[:, t, :], stats[:, t, :, :]))
            r, h, u = rr[:, ts], varh[:, ts], newton[:, ts]
            link(lambda e: e.tensor_scalar(h, mv[:, ts, 1], EPS, 0.5, ALU.add, ALU.mult))
            link(lambda e: e.tensor_scalar(r.bitcast(I32), h.bitcast(I32), -0.5, GUESS, ALU.mult, ALU.add))
            for _ in range(NEWTON_STEPS):
                link(lambda e: e.tensor_tensor(u, r, r, ALU.mult))
                link(lambda e: e.tensor_tensor(u, u, h, ALU.mult))
                link(lambda e: e.scalar_tensor_tensor(out=r, in0=u, scalar=1.5, in1=r, op0=ALU.subtract, op1=ALU.mult))
            dve.do(lambda e: e.scalar_tensor_tensor(out=nmr[:, ts], in0=mv[:, ts, 0], scalar=-1.0, in1=r,
                                                    op0=ALU.mult, op1=ALU.mult), (norm, b, t0, "std"))

        def scale_row(norm, b, t0, t, dst, src, *names):
            _, rr, nmr = norms[norm]
            act.wait(norm, b, t0, "std")
            act.do(lambda e: e.activation(dst, src, ACT.Identity, bias=nmr[:, t:t + 1], scale=rr[:, t:t + 1]), *names)

        def row_stats(norm, b, t, halves):
            for i, half in enumerate(halves):
                dve.do(lambda e, i=i, half=half: e.bn_stats(stats[:, t, i, :], half), ("stats", norm, b, t, i))

        def load_x(b, t):
            if b >= 2:
                sp.wait("stored", b - 2, t)
            elif b:
                sp.wait("x turned", 0, KD - 1)
            sp.dma(work[t][:, :], x[b * TB + t], s_work[t], counts, ("x", b, t))

        def next_x(b, t):
            if b + 2 < NB:
                load_x(b + 2, t)

        def x_stats(b, t):
            dve.wait("x", b, t)
            row_stats("ln1", b, t, [work[t][:, 0:512], work[t][:, 512:1024]])

        def next_x_stats(b, t):
            if b + 2 < NB:
                x_stats(b + 2, t)

        def scale_x(b, t):
            if t < TB // 2:
                scale_row("ln1", b, 0, t, work[t][:, :], work[t][:, :], ("ln1", b, t))
            else:
                _, rr, nmr = norms["ln1"]
                dve.wait("ln1", b, 0, "std")
                dve.do(lambda e: e.tensor_scalar(work[t][:, :], work[t][:, :], rr[:, t:t + 1], nmr[:, t:t + 1], ALU.mult, ALU.add),
                       ("ln1", b, t))

        def filt_of(b, kt):
            return v[:, 0, :].rearrange("p (j n) -> p j n", j=FILT) if b == 0 and kt % 2 else filt[:, :, :]

        turned = {}

        def turn_x(b, kt):
            pe.wait("ident")
            n, dst = take("turn")
            for t in range(TB):
                pe.wait("ln1", b, t)
                names = [("x turned", b, kt)] if t == TB - 1 else []
                pe.do(lambda e, t=t: e.transpose(dst[:, t * P:(t + 1) * P], work[t][:, kt * P:(kt + 1) * P], ident[:, :]), *names)
            turned[b, kt] = n, dst

        def copy_x(b, kt):
            n, dst = turned[b, kt]
            act.wait("x turned", b, kt)
            if b or kt >= 2:
                for j in range(FILT):
                    act.wait("filt", *back(KD, b, kt, 2), j)
            act.do(lambda e: e.activation(xt[kt % 2][:, 1:L + 1], dst[:, :], ACT.Copy), ("xt", b, kt), ("turn read", n))

        def filter_x(b, kt):
            i, buf = kt % 2, filt_of(b, kt)
            d = [xt[i][:, a:a + L - 1:2] for a in range(4)]
            terms = [(0, 2, ALU.subtract), (1, 2, ALU.add), (2, 1, ALU.subtract), (1, 3, ALU.subtract)]
            for j, (p, q, op) in enumerate(terms):
                eng = dve if j >= 2 else pool
                eng.wait("xt", b, kt)
                eng.wait("pad", i, L + 1)
                if b and (b > 1 or kt):
                    eng.wait("f lo", *back(KD, b, kt, 1))
                elif b or kt >= 2:
                    eng.wait("f lo", *back(KD, b, kt, 2))
                eng.do(lambda e, j=j, p=p, q=q, op=op: e.tensor_tensor(buf[:, j, :], d[p], d[q], op), ("filt", b, kt, j))

        def x_hi(b, kt):
            if b:
                act.wait("conv", b - 1, C_ORDER[-1])
            for j in range(FILT):
                act.wait("filt", b, kt, j)
            act.do(lambda e: e.activation(f_hi[:, kt, :, :], filt_of(b, kt), ACT.Copy), ("f hi", b, kt))

        def x_lo(b, kt):
            dve.wait("f hi", b, kt)
            dve.do(lambda e: e.tensor_tensor(f_lo[:, kt, :, :], filt_of(b, kt), f_hi[:, kt, :, :].bitcast(F32), ALU.subtract),
                   ("f lo", b, kt))

        def back(size, b, i, by):
            return divmod(b * size + i - by, size)

        def conv(b, turn, slot):
            c = C_ORDER[turn]
            j, half = order_of(b, turn)[slot]
            outer_bank, inner_bank = conv_banks[turn % 2]
            m3_bank, m2_bank = banks_of["side"] if b == 0 and turn == 0 else (outer_bank, inner_bank)
            if slot == 0:
                if turn >= 2:
                    pe.wait("conv read", b, turn - 2)
                elif turn == 1:
                    drained("stream")
                elif b:
                    for g in range(2):
                        pe.wait("scores read", b - 1, HP - 1, g)
            acc = (outer_bank[:, 0:L2], inner_bank[:, 0:L2], m2_bank[:, L2:L], m3_bank[:, L2:L])[j]
            k, wh, wl = use_chunk("conv", b, c, j, half)
            for i in range(HALF):
                kt = half * HALF + i
                pe.wait("f lo", b, kt)
                last = half == HALVES - 1 and i == HALF - 1
                names = [("chunk used", k)] if i == HALF - 1 else []
                names += [("conv", b, c)] if last and slot == SLOTS - 1 else []
                cols = slice(i * P, (i + 1) * P)
                mm3(acc, wh[:, cols], wl[:, cols], f_hi[:, kt, j, :], f_lo[:, kt, j, :], half == 0 and i == 0, last, *names)
            if slot == SLOTS - 1:
                combine(b, turn, c, outer_bank, inner_bank, m2_bank, m3_bank)

        def combine(b, turn, c, outer_bank, inner_bank, m2_bank, m3_bank):
            def out_of_psum():
                act.wait("conv", b, c)
                if turn:
                    act.wait("m12 sums", b, C_ORDER[turn - 1], 1)
                elif b:
                    act.wait("scores", b - 1, HP - 1, 1)
                else:
                    act.wait("lora lo", 1)
                if m2_bank is inner_bank:
                    act.do(lambda e: e.activation(m12, inner_bank[:, :].rearrange("p (j n) -> p j n", j=2), ACT.Copy), ("m12", b, c))
                else:
                    act.do(lambda e: e.activation(m12[:, 0, :], inner_bank[:, 0:L2], ACT.Copy))
                    act.do(lambda e: e.activation(m12[:, 1, :], m2_bank[:, L2:L], ACT.Copy), ("m12", b, c))
                if turn:
                    pool.wait("conv read", b, turn - 1)
                pool.wait("m12", b, c)
                for i, op in enumerate((ALU.add, ALU.subtract)):
                    pool.do(lambda e, i=i, op=op: e.tensor_tensor(m12_sums[:, i, :], m12[:, 0, :], m12[:, 1, :], op),
                            ("m12 sums", b, c, i))

            def add_up():
                if turn:
                    dve.wait("c", b, C_ORDER[turn - 1])
                elif b:
                    dve.wait("prob turned", b - 1, HP - 1, 1)
                dve.wait("small")
                dve.wait("m12 sums", b, c, 0)
                dve.do(lambda e: e.scalar_tensor_tensor(out=conv_out[:, 0:L:2], in0=outer_bank[:, 0:L2], scalar=conv_bias(c),
                                                        in1=m12_sums[:, 0, :], op0=ALU.add, op1=ALU.add), ("even", b, c))
                dve.wait("m12 sums", b, c, 1)
                dve.do(lambda e: e.scalar_tensor_tensor(out=conv_out[:, 1:L:2], in0=m12_sums[:, 1, :], scalar=conv_bias(c),
                                                        in1=m3_bank[:, L2:L], op0=ALU.add, op1=ALU.subtract), ("conv read", b, turn))

            def split_up():
                if b:
                    act.wait(*(("qk", b - 1, HP - 1) if c < 2 * KW else ("v full", b - 1, 1, TB - 1)))
                act.wait("conv read", b, turn)
                act.do(lambda e: e.activation(c_hi[:, c, :], conv_out, ACT.Copy), ("c hi", b, c))
                dve.wait("c hi", b, c)
                dve.do(lambda e: e.tensor_tensor(c_lo[:, c, :], conv_out, c_hi[:, c, :].bitcast(F32), ALU.subtract), ("c", b, c))

            later(1, out_of_psum)
            later(2, add_up)
            later(3, split_up)

        def split_out(n, acc, hi, lo, bias_col, ready, done):
            act.wait(*ready)
            act.do(lambda e: e.activation(hi, acc, ACT.Identity, bias=bias_col), ("hi of",) + done)
            dve.wait("hi of", *done)
            names = [done] + ([("stream read", n)] if n is not None else [])
            dve.do(lambda e: e.scalar_tensor_tensor(out=lo, in0=acc, scalar=bias_col, in1=hi.bitcast(F32),
                                                    op0=ALU.add, op1=ALU.subtract), *names)

        def project_v(b, n, t):
            if n == 0 and t == 0:
                pe.wait("conv read", b, NC - 2)
            kind = "turn" if n else "v"
            u, acc = take(kind)
            toks = slice(t * P, (t + 1) * P)
            for kt in range(KW):
                k, wh, wl = use_chunk("v", b, n, kt)
                c = 2 * KW + kt
                pe.wait("c", b, c)
                names = [("v full", b, n, t)] if kt == KW - 1 else []
                names += [("chunk used", k)] if t == TB - 1 else []
                mm3(acc[:, :], c_hi[:, c, toks], c_lo[:, c, toks], wh[:, :], wl[:, :], kt == 0, kt == KW - 1, *names)
            act.wait("v full", b, n, t)
            if b:
                act.wait("moe out", b - 1, t)
            act.do(lambda e: e.activation(v[:, t, n * 512:(n + 1) * 512], acc[:, :], ACT.Copy),
                   ("v", b, n, t), (kind + " read", u))

        def project_qk(b, h, j):
            if h == 0:
                pe.wait("conv read", b, NC - 1)
            k, wh, wl = use_chunk("qk", b, h)
            n, acc = take("stream")
            for kt in range(KW):
                c = j * KW + kt
                pe.wait("c", b, c)
                cols = slice((j * KW + kt) * P, (j * KW + kt + 1) * P)
                names = [("qk part", b, h, j)] if kt == KW - 1 else []
                names += [("qk", b, h), ("chunk used", k)] if kt == KW - 1 and j == 1 else []
                mm3(acc[:, :], wh[:, cols], wl[:, cols], c_hi[:, c, :], c_lo[:, c, :], kt == 0, kt == KW - 1, *names)
            eng = dve if j else act
            eng.wait("qk part", b, h, j)
            if h:
                eng.wait("scores", b, h - 1, 1)
            if j:
                dve.do(lambda e: e.tensor_scalar(k_t[:, :], acc[:, :], head_bias(1, h), None, ALU.add),
                       ("qk sb", b, h, 1), ("stream read", n))
            else:
                act.do(lambda e: e.activation(q_t[:, :], acc[:, :], ACT.Identity, bias=head_bias(0, h)),
                       ("qk sb", b, h, 0), ("stream read", n))

        def scores(b, h):
            if h == 0:
                drained("v")
            for g in range(2):
                rows = slice(g * DH, (g + 1) * DH)
                pe.wait("qk sb", b, h, 0)
                pe.wait("qk sb", b, h, 1)
                if h:
                    pe.wait("scores read", b, h - 1, g)
                for t in range(TB):
                    toks = slice(t * P, (t + 1) * P)
                    mm(score_banks[g][:, toks], q_t[rows, toks], k_t[rows, toks], True, True,
                       *([("scores", b, h, g)] if t == TB - 1 else []))
            for g in range(2):
                dve.wait("scores", b, h, g)
                if h:
                    dve.wait("prob turned", b, h - 1, g)
                for t in range(TB):
                    dve.do(lambda e, g=g, t=t: e.tensor_tensor_reduce(
                        prob[:, g, t, :], score_banks[g][:, t * P:(t + 1) * P], mask[:, :], 1.0, NEG_INF * 4,
                        ALU.add, ALU.max, top[:, g, t:t + 1]), *([("scores read", b, h, g)] if t == TB - 1 else []))
                dve.wait("scores read", b, h, g)
                dve.do(lambda e, g=g: e.tensor_scalar(ntop[:, g, :], top[:, g, :], -QK_SCALE, None, ALU.mult),
                       ("ntop", b, h, g))

        def exponentials(b, h, g, ts):
            act.wait("ntop", b, h, g)
            for t in ts:
                act.do(lambda e, t=t: e.activation(prob[:, g, t, :], prob[:, g, t, :], ACT.Exp,
                                                   bias=ntop[:, g, t:t + 1], scale=QK_SCALE,
                                                   accum_out=total[:, g, t:t + 1]),
                       *([("exp", b, h, g)] if t == TB - 1 else []))

        def normalise(b, h, g):
            dve.wait("exp", b, h, g)
            dve.do(lambda e: e.reciprocal(rtotal[:, g, :], total[:, g, :]), ("rtotal", b, h, g))
            pool.wait("rtotal", b, h, g)
            pool.do(lambda e: e.tensor_tensor(
                prob[:, g, :, :], prob[:, g, :, :],
                rtotal[:, g, :].rearrange("p (t o) -> p t o", o=1).broadcast_to([P, TB, P]), ALU.mult),
                ("prob", b, h, g))

        def turn_prob(b, h):
            for g in range(2):
                n, dst = take("turn")
                pe.wait("prob", b, h, g)
                for t in range(TB):
                    pe.do(lambda e, g=g, t=t, dst=dst: e.transpose(dst[:, t * P:(t + 1) * P], prob[:, g, t, :], ident[:, :]),
                          *([("prob turned", b, h, g)] if t == TB - 1 else []))
                dve.wait("prob turned", b, h, g)
                if h:
                    dve.wait("pv part", b, h - 1, g)
                dve.do(lambda e, g=g, dst=dst: e.tensor_copy(prob_t[:, g, :], dst[:, :]), ("prob t", b, h, g), ("turn read", n))

        def attend(b, h):
            n, acc = take("stream")
            for g in range(2):
                pe.wait("prob t", b, h, g)
                for t in range(TB):
                    pe.wait("v", b, (2 * h + g) * DH // 512, t)
                    names = [("pv part", b, h, g)] if t == TB - 1 else []
                    names += [("pv", b, h)] if t == TB - 1 and g == 1 else []
                    head = (2 * h + g) * DH
                    mm(acc[g * DH:(g + 1) * DH, t * P:(t + 1) * P], v[:, t, head:head + DH],
                       prob_t[:, g, t * P:(t + 1) * P], True, True, *names)
            if h:
                act.wait("wo", b, h - 1)
            split_out(n, acc[:, :], o_hi[:, :], o_lo[:, :], head_bias(2, h), ("pv", b, h), ("o", b, h))

        def project_wo(b, h):
            if h == 0:
                drained("side")
            k, wh, wl = use_chunk("wo", b, h)
            pe.wait("o", b, h)
            for m in range(KW):
                cols = slice(m * P, (m + 1) * P)
                names = [("wo", b, h), ("chunk used", k)] if m == KW - 1 else []
                mm3(wo_banks[m][:, :], wh[:, cols], wl[:, cols], o_hi[:, :], o_lo[:, :], h == 0, h == HP - 1, *names)

        def finish_wo(b):
            for m in range(KW):
                split_out(None, wo_banks[m][:, :], po_hi[:, m, :], po_lo[:, m, :], out_bias(m),
                          ("wo", b, HP - 1), ("po", b, m))

        def load_residual(b, t):
            if b + 1 < NB:
                sp.wait("x turned", b + 1, KD - 1)
            sp.dma(work[t][:, :], x[b * TB + t], s_work[t], counts, ("residual", b, t))

        def project_out(b, t0, n, kind="side", lag=0):
            for t in (t0, t0 + 1):
                u, acc = take(kind)
                toks = slice(t * P, (t + 1) * P)
                for kt in range(KW):
                    k, wh, wl = use_chunk("proj", b, t0, n, kt)
                    pe.wait("po", b, kt)
                    names = [("proj", b, t, n)] if kt == KW - 1 else []
                    names += [("chunk used", k)] if t == t0 + 1 else []
                    mm3(acc[:, :], po_hi[:, kt, toks], po_lo[:, kt, toks], wh[:, :], wl[:, :], kt == 0, kt == KW - 1, *names)
                if lag:
                    later(lag, lambda t=t, acc=acc, u=u: add_proj_bias(b, t, n, acc, (kind + " read", u)))
                else:
                    add_proj_bias(b, t, n, acc, (kind + " read", u))

        def add_proj_bias(b, t, n, acc, read):
            dve.wait("proj", b, t, n)
            dve.wait("pv", b, HP - 1)
            half = y[t][:, n * 512:(n + 1) * 512]
            dve.do(lambda e: e.tensor_tensor(half, acc[:, :], projb[:, n * 512:(n + 1) * 512], ALU.add),
                   ("attn out", b, t, n), read)
            dve.wait("attn out", b, t, n)
            dve.do(lambda e: e.bn_stats(stats[:, t, n, :], half), ("stats", "ln2", b, t, n))

        def adder(b, t):
            return dve if b == NB - 1 and t % 2 else pool

        def add_norm2(b, t0):
            inverse_std("ln2", b, t0, PR)

            def add_up():
                for t in (t0, t0 + 1):
                    scale_row("ln2", b, t0, t, y[t], y[t], ("ln2", b, t))
                    eng = adder(b, t)
                    eng.wait("residual", b, t)
                    eng.wait("ln2", b, t)
                    eng.do(lambda e, t=t: e.tensor_tensor(work[t][:, :], work[t][:, :], y[t], ALU.add), ("x1", b, t))
            later(1, add_up)

        def norm3(b, t0, lag=NORM3_LAG):
            for t in (t0, t0 + 1):
                dve.wait("x1", b, t)
                row_stats("ln3", b, t, [work[t][:, 0:512], work[t][:, 512:1024]])
            inverse_std("ln3", b, t0, PR)

            def scale():
                for t in (t0, t0 + 1):
                    scale_row("ln3", b, t0, t, y[t], work[t][:, :], ("ln3", b, t))
            later(lag, scale)

        def lora_mid(b, t):
            pe.wait("ln3", b, t)
            for half in range(2):
                n, dst = take("turn")
                for i in range(4):
                    kt = half * 4 + i
                    pe.do(lambda e, i=i, kt=kt, dst=dst: e.transpose(dst[:, i * P:(i + 1) * P], y[t][:, kt * P:(kt + 1) * P], ident[:, :]),
                          *([("x3 turned", b, t, half)] if i == 3 else []))
                act.wait("x3 turned", b, t, half)
                if t:
                    act.wait("mid", b, t - 1)
                act.do(lambda e, half=half, dst=dst: e.activation(x3_t[:, half * 4:(half + 1) * 4, :],
                                                                  dst[:, :].rearrange("p (k n) -> p k n", n=P), ACT.Copy),
                       ("x3_t", b, t, half), ("turn read", n))

        def back_pair(b, t):
            n, i = back(TB // PR, b, t // PR, 1)
            return n, i * PR

        def lora_mid2(b, t):
            i = t % PR
            n, acc = take("side")
            for kt in range(KD):
                pe.wait("x3_t", b, t, kt // 4)
                mm(acc[:, 0:ER + E], x3_t[:, kt, :], aw_sb[:, kt, :], kt == 0, kt == KD - 1,
                   *([("mid", b, t)] if kt == KD - 1 else []))

            def out_of_psum():
                dve.wait("mid", b, t)
                if (b, t) >= (0, PR):
                    dve.wait("mid2", *back_pair(b, t))
                dve.do(lambda e: e.tensor_copy(mid[:, i, :], acc[:, 0:ER]))
                dve.do(lambda e: e.tensor_copy(logits[:, i, :], acc[:, ER:ER + E]), ("logits", b, t), ("side read", n))
            later(1, out_of_psum)

        def gates(b, t0):
            wide = [P, PR, E, E]
            own = logits[:, :, :].rearrange("p t (i o) -> p t i o", o=1).broadcast_to(wide)
            other = logits[:, :, :].rearrange("p t (o j) -> p t o j", o=1).broadcast_to(wide)
            spread = lambda a, n: a[:, :].rearrange("p (t o) -> p t o", o=1).broadcast_to([P, PR, n])
            for t in range(t0, t0 + PR):
                dve.wait("logits", b, t)
            link(lambda e: e.tensor_reduce(gtop[:, :], logits[:, :, :], AX.X, ALU.max))
            dve.do(lambda e: e.tensor_tensor(gexp[:, :, :], logits[:, :, :], spread(gtop, E), ALU.subtract), ("shifted", b, t0))
            act.wait("shifted", b, t0)
            act.do(lambda e: e.activation(gexp[:, :, :], gexp[:, :, :], ACT.Exp), ("gexp", b, t0))
            dve.do(lambda e: e.tensor_tensor(above[:, :, :, :], other, own, ALU.is_gt))
            link(lambda e: e.tensor_tensor(tied[:, :, :, :], other, own, ALU.is_equal))
            link(lambda e: e.tensor_tensor(tied[:, :, :, :], tied[:, :, :, :], before[:, :, :, :], ALU.mult))
            link(lambda e: e.tensor_tensor(above[:, :, :, :], above[:, :, :, :], tied[:, :, :, :], ALU.add))
            link(lambda e: e.tensor_reduce(rank[:, :, :], above[:, :, :, :], AX.X, ALU.add))
            dve.wait("gexp", b, t0)
            link(lambda e: e.scalar_tensor_tensor(out=gate[:, :, :], in0=rank[:, :, :], scalar=float(TOP_K), in1=gexp[:, :, :],
                                                  op0=ALU.is_lt, op1=ALU.mult))
            link(lambda e: e.tensor_reduce(gsum[:, :], gate[:, :, :], AX.X, ALU.add))
            link(lambda e: e.reciprocal(gsum[:, :], gsum[:, :]))
            link(lambda e: e.scalar_tensor_tensor(out=gate[:, :, :], in0=gate[:, :, :], scalar=LORA_SCALE, in1=spread(gsum, E),
                                                  op0=ALU.mult, op1=ALU.mult))
            by_expert = mid[:, :, :].rearrange("p t (e r) -> p t e r", r=R)
            link(lambda e: e.tensor_tensor(by_expert, by_expert, gate[:, :, :].rearrange("p t (e o) -> p t e o", o=1)
                                           .broadcast_to([P, PR, E, R]), ALU.mult))
            link(lambda e: e.tensor_copy(mid2[:, :, 0:ER], mid[:, :, :]))
            dve.do(lambda e: e.tensor_tensor(mid2[:, :, ER:2 * ER], mid[:, :, :], mid2[:, :, 0:ER].bitcast(F32), ALU.subtract),
                   ("mid2", b, t0))

        def turn_mid(b, t0):
            n, dst = take("turn")
            pe.wait("mid2", b, t0)
            for i in range(PR):
                pe.do(lambda e, i=i: e.transpose(dst[:, i * P:(i + 1) * P], mid2[:, i, :].bitcast(F32), ident[:, :]),
                      *([("mid turned", b, t0)] if i == PR - 1 else []))
            act.wait("mid turned", b, t0)
            act.do(lambda e: e.activation(mid_t[:, :, :], dst[:, 0:PR * P].rearrange("p (t n) -> p t n", n=P), ACT.Copy),
                   ("mid_t", b, t0), ("turn read", n))

        def lora_out(b, t0, kinds=("side", "turn")):
            pe.wait("mid_t", b, t0)
            pe.wait("lora lo", 1)
            accs = {}
            for t, kind in zip((t0, t0 + 1), kinds):
                for j in range(2):
                    u, acc = take(kind)
                    accs[t, j] = acc, (kind + " read", u)
                    cols = slice(j * 512, (j + 1) * 512)
                    mm(acc[:, :], mid_t[:, t % PR, :], lora_b[0][:, cols], True, False)
                    mm(acc[:, :], mid_t[:, t % PR, :], lora_b[1][:, cols], False, True, ("delta", b, t, j))
            for (t, j), (acc, _) in accs.items():
                dve.wait("delta", b, t, j)
                dve.do(lambda e, t=t, j=j, acc=acc: e.bn_stats(stats[:, t, j, :], acc[:, :]), ("stats", "ln4", b, t, j))
            inverse_std("ln4", b, t0, PR)

            def scale():
                for (t, j), (acc, read) in accs.items():
                    scale_row("ln4", b, t0, t, y[t][:, j * 512:(j + 1) * 512], acc[:, :], ("ln4", b, t, j), read)
                for t in (t0, t0 + 1):
                    eng = adder(b, t)
                    eng.wait("ln4", b, t, 1)
                    eng.do(lambda e, t=t: e.tensor_tensor(work[t][:, :], work[t][:, :], y[t], ALU.add), ("moe out", b, t))
                later(STORE_LAG, store)

            def store():
                for t in (t0, t0 + 1):
                    sp.wait("moe out", b, t)
                    sp.dma(out[b * TB + t], work[t][:, :], s_out[t], counts, ("stored", b, t))

            later(OUT_LAG, scale)

        SIDE = [
            (9, project_out, 0, 0), (9, project_out, 0, 1), (10, project_out, 2, 0), (11, add_norm2, 0), (11, project_out, 2, 1),
            (16, add_norm2, 2), (16, norm3, 0), (20, lora_mid, 0), (23, norm3, 2), (23, lora_mid2, 0),
            (23, lora_mid, 1), (25, lora_mid2, 1), (26, lora_mid, 2), (28, gates, 0), (28, lora_mid2, 2),
            (29, lora_mid, 3), (30, turn_mid, 0), (31, lora_mid2, 3), (33, lora_out, 0), (35, gates, 2),
            (37, turn_mid, 2), (38, lora_out, 2), (38, next_x, 0), (38, next_x, 1), (43, next_x, 2),
            (44, next_x_stats, 0), (44, next_x_stats, 1), (44, next_x, 3), (46, next_x_stats, 2),
        ]

        TAIL = [
            (project_out, 0, 0), (project_out, 0, 1), (add_norm2, 0), (project_out, 2, 0, "stream", 0), (tick,),
            (norm3, 0, 3), (project_out, 2, 1, "turn", 2), (tick,), (tick,), (tick,), (lora_mid, 0), (lora_mid2, 0),
            (add_norm2, 2), (tick,), (lora_mid, 1), (norm3, 2, 2), (tick,), (lora_mid2, 1), (tick,), (gates, 0),
            (lora_mid, 2), (lora_mid2, 2), (lora_mid, 3), (lora_mid2, 3), (tick,), (turn_mid, 0), (gates, 2),
            (lora_out, 0, ("side", "v")), (turn_mid, 2), (lora_out, 2, ("stream", "turn")),
        ]

        def side(b):
            plan = {}
            for s, f, *args in SIDE:
                if b < 0 and f not in (next_x, next_x_stats):
                    continue
                plan.setdefault(s, []).append((f, (b, *args)))
            return plan

        FILL = {HP: 3, HP + 1: 2, HP + 2: 3}
        ALL = NC * SLOTS

        def order_of(b, turn):
            if b == 0 and turn == 0:
                return [(j, half) for half in range(HALVES) for j in J_ORDER]
            return [(j, half) for j in J_ORDER for half in range(HALVES)]

        def chunk_order():
            names = []

            def conv_names(b, a, z):
                for s in range(a, z):
                    names.append(("conv", b, C_ORDER[s // SLOTS], *order_of(b, s // SLOTS)[s % SLOTS]))
                    for f, args in side(b - 1).get(s, []):
                        if f is project_out:
                            names.extend(("proj",) + args + (kt,) for kt in range(KW))

            done = 0
            for b in range(NB):
                conv_names(b, done, ALL)
                done = 0
                names.extend(("v", b, 0, kt) for kt in range(KW))
                for i in range(HP + LAG):
                    if i >= LAG:
                        names.append(("wo", b, i - LAG))
                    if i == 0:
                        names.extend(("v", b, 1, kt) for kt in range(KW))
                    if i < HP:
                        names.append(("qk", b, i))
                    if b + 1 < NB and i in FILL:
                        conv_names(b + 1, done, done + FILL[i])
                        done += FILL[i]
            for f, *args in TAIL:
                if f is project_out:
                    names.extend(("proj", NB - 1, *args[:2], kt) for kt in range(KW))
            return names

        def conv_chunks(b, a, z):
            plan = side(b - 1)
            for s in range(a, z):
                tick()
                conv(b, s // SLOTS, s % SLOTS)
                for f, args in plan.get(s, []):
                    f(*args)

        order = chunk_order()
        plan_chunks(order)
        number.update((name, k) for k, name in enumerate(order))
        for t in range(TB):
            load_x(0, t)
        constants()
        load_chunks()
        setup()
        for t in range(TB):
            x_stats(0, t)
        inverse_std("ln1", 0, 0, TB)
        for t in range(TB):
            scale_x(0, t)
        act.wait("small")
        for kt in range(KD):
            turn_x(0, kt)
            copy_x(0, kt)
            if kt:
                x_hi(0, kt - 1)
            filter_x(0, kt)
            if kt:
                x_lo(0, kt - 1)
            if kt > HALF:
                conv(0, 0, kt - HALF - 1)
            elif kt == 0:
                split_chunks(1)
        x_hi(0, KD - 1)
        x_lo(0, KD - 1)
        done = HALF - 1
        lora_weights()
        dve.wait("small")
        dve.wait("mask")
        dve.wait("before", E - 1)
        pe.wait("small")

        for b in range(NB):
            conv_chunks(b, done, ALL)
            done = 0
            more = b + 1 < NB
            for t in range(TB):
                tick()
                project_v(b, 0, t)
                if more and t == 3:
                    x_stats(b + 1, TB - 1)
                    inverse_std("ln1", b + 1, 0, TB)
            settle()
            for i in range(HP + LAG):
                if i >= LAG:
                    project_wo(b, i - LAG)
                if more and 2 <= i <= HP:
                    x_hi(b + 1, i - 1)
                if 2 <= i < HP + 2:
                    turn_prob(b, i - 2)
                if 1 <= i <= HP:
                    scores(b, i - 1)
                    exponentials(b, i - 1, 0, range(TB // 2))
                if 2 <= i < HP + 2:
                    attend(b, i - 2)
                if more and 2 <= i < HP:
                    turn_x(b + 1, i)
                if 1 <= i <= HP:
                    exponentials(b, i - 1, 0, range(TB // 2, TB))
                    normalise(b, i - 1, 0)
                    if more and i > 1:
                        x_lo(b + 1, i - 1)
                    exponentials(b, i - 1, 1, range(TB))
                    if more and 2 <= i < HP:
                        copy_x(b + 1, i)
                    normalise(b, i - 1, 1)
                for t in ([0], range(1, TB), [])[min(i, 2)]:
                    project_v(b, 1, t)
                    if more and t == 2:
                        turn_x(b + 1, 0)
                        copy_x(b + 1, 0)
                        filter_x(b + 1, 0)
                    if more and t == 3:
                        x_hi(b + 1, 0)
                        x_lo(b + 1, 0)
                        turn_x(b + 1, 1)
                        copy_x(b + 1, 1)
                if i < HP:
                    project_qk(b, i, 0)
                    project_qk(b, i, 1)
                    if more and i:
                        filter_x(b + 1, i)
                if i == 0 and more:
                    for t in range(TB):
                        scale_x(b + 1, t)
                if b + 1 < NB and i in FILL:
                    conv_chunks(b + 1, done, done + FILL[i])
                    done += FILL[i]
            finish_wo(b)
            for t in range(TB):
                load_residual(b, t)
        b = NB - 1
        for step, *args in TAIL:
            step(*args) if step is tick else step(b, *args)
        settle()
        for t in range(TB):
            sp.wait("stored", b, t)

        with nc.Block() as block:
            block.tensor(pe.emit)
            block.scalar(act.emit)
            block.vector(dve.emit)
            block.gpsimd(pool.emit)
            block.sync(sp.emit)


def kernel(**inputs):
    import numpy as np
    import concourse.bacc as bacc
    from concourse.bass_utils import run_bass_kernel_spmd

    g = {k.replace("L0_attn_", "").replace("L0_ffn_", ""): np.asarray(a) for k, a in inputs.items()}
    flat = lambda a, *s: np.ascontiguousarray(a.reshape(*s))
    columns = lambda a: a.reshape(-1, P).T
    arrays = {
        "x": flat(g["inputs"], NB * TB, P, D),
        "conv_w": flat(g["conv_w"], TAPS, D, 3 * W),
        "wq": flat(g["wq"], W, H * DH),
        "wk": flat(g["wk"], W, H * DH),
        "wv": flat(g["wv"], W, H * DH),
        "wo": flat(g["wo"], H * DH, W),
        "proj_w": flat(g["proj_w"], W, D),
        "biases": np.ascontiguousarray(np.concatenate([columns(g[n]) for n in ("conv_b", "bq", "bk", "bv", "bo")], axis=1)),
        "proj_b": np.ascontiguousarray(np.broadcast_to(g["proj_b"], (P, D))),
        "aw": np.ascontiguousarray(np.concatenate([g["A"].reshape(ER, D).T, g["Wr"].T], axis=1)),
        "b_t": np.ascontiguousarray(g["B"].transpose(0, 2, 1).reshape(ER, D)),
    }
    nc = bacc.Bacc("TRN2", target_bir_lowering=False, num_devices=1)
    aps = {n: nc.dram_tensor(n, a.shape, mybir.dt.from_np(a.dtype), kind="ExternalInput").ap() for n, a in arrays.items()}
    out = nc.dram_tensor("out", (NB * TB, P, D), F32, kind="ExternalOutput").ap()
    build(nc, out=out, **aps)
    result = run_bass_kernel_spmd(nc, [arrays], core_ids=[0]).results[0]["out"]
    return result.reshape(NB, L, D)
```
